# Optimizing a Trainium2 kernel written in Bass

```python
import numpy as np
import jax
import jax.numpy as jnp

def _softmax(x, axis=-1):
    return jax.nn.softmax(x, axis=axis)

def _gelu(x):
    return jax.nn.gelu(x, approximate=True)

def _silu(x):
    return jax.nn.silu(x)

def _sigmoid(x):
    return jax.nn.sigmoid(x)

def _layernorm(x, axis=-1, eps=1e-05):
    m = jnp.mean(x, axis=axis, keepdims=True)
    v = jnp.var(x, axis=axis, keepdims=True)
    return (x - m) / jnp.sqrt(v + eps)

def _scatter_add(tgt, idx, src, axis=0):
    return tgt.at[idx].add(src)

def _segment_sum(src, seg, n):
    return jax.ops.segment_sum(src, seg, n)
kernel_name = 'mk_adj_preln_d2_adj_r2_e63b28'

def setup_inputs(seed: int=0):
    np.random.seed(seed)
    _w = jnp.asarray

    def _rec_inputs():
        import jax
        import jax.numpy as jnp
        _gk = jax.random.key(seed)
        x = -0.0001538 + 1 * jax.random.normal(jax.random.fold_in(_gk, 1), (32, 256, 384), jnp.float32)
        _a = jax.random.bernoulli(jax.random.fold_in(_gk, 2), 0.0078125, (32, 256, 256))
        _a = jnp.logical_or(_a, jnp.eye(256, dtype=bool))
        adj = _a
        return (x, adj)
    x, adj = _rec_inputs()

    def _L0_gnn_setup():
        import jax, jax.numpy as jnp
        import numpy as np
        B, S, H = (4, 1024, 384)
        NUM_HEADS = 6
        HEAD_SIZE = H // NUM_HEADS
        NEG = -9000000000000000.0

        def _heads(x):
            b, s, _ = x.shape
            return x.reshape(b, s, NUM_HEADS, HEAD_SIZE).transpose(0, 2, 1, 3)
        key = jax.random.key(seed)
        ks = jax.random.split(key, 10)
        seq_inputs = jax.random.normal(ks[0], (B, S, H), dtype=jnp.float32)
        gm = jax.random.randint(ks[1], (B, S, S), 0, 2) > 0
        graph_mask = gm | jnp.eye(S, dtype=bool)[None]
        sc = 1.0 / np.sqrt(H)
        Wq = jax.random.normal(ks[2], (H, H), dtype=jnp.float32) * sc
        bq = jnp.zeros((H,), dtype=jnp.float32)
        Wk = jax.random.normal(ks[3], (H, H), dtype=jnp.float32) * sc
        bk = jnp.zeros((H,), dtype=jnp.float32)
        Wv = jax.random.normal(ks[4], (H, H), dtype=jnp.float32) * sc
        bv = jnp.zeros((H,), dtype=jnp.float32)
        Wf = jax.random.normal(ks[5], (H, H), dtype=jnp.float32) * sc
        bf = jnp.zeros((H,), dtype=jnp.float32)
        return {'seq_inputs': seq_inputs, 'Wq': Wq, 'bq': bq, 'Wk': Wk, 'bk': bk, 'Wv': Wv, 'bv': bv, 'Wf': Wf, 'bf': bf, 'graph_mask': graph_mask}
    _L0_gnn_all = _L0_gnn_setup()
    _L0_gnn_in = {k: v for k, v in _L0_gnn_all.items() if k in ('Wq', 'bq', 'Wk', 'bk', 'Wv', 'bv', 'Wf', 'bf')}
    del _L0_gnn_all

    def _L1_gnn_setup():
        import jax, jax.numpy as jnp
        import numpy as np
        ATT_HEAD = 12
        IN_DIM = 384
        OUT_DIM = IN_DIM // ATT_HEAD
        LEAKY_ALPHA = 0.2
        B, N = (8, 256)
        key = jax.random.key(seed)
        ks = jax.random.split(key, 8)
        feat_in = jax.random.normal(ks[0], (B, N, IN_DIM), dtype=jnp.float32)
        adj = jax.random.randint(ks[1], (B, N, N), 0, 2) > 0
        lim_W = float(np.sqrt(6.0 / (IN_DIM + OUT_DIM)))
        W = jax.random.uniform(ks[2], (ATT_HEAD, IN_DIM, OUT_DIM), minval=-lim_W, maxval=lim_W, dtype=jnp.float32)
        b = jnp.zeros((OUT_DIM,), dtype=jnp.float32)
        lim_w = float(np.sqrt(6.0 / (OUT_DIM + 1)))
        w_src = jax.random.uniform(ks[3], (ATT_HEAD, OUT_DIM, 1), minval=-lim_w, maxval=lim_w, dtype=jnp.float32)
        w_dst = jax.random.uniform(ks[4], (ATT_HEAD, OUT_DIM, 1), minval=-lim_w, maxval=lim_w, dtype=jnp.float32)
        std_H = float(np.sqrt(2.0 / (IN_DIM + IN_DIM)))
        H_w = jax.random.normal(ks[5], (IN_DIM, IN_DIM), dtype=jnp.float32) * std_H
        H_b = jax.random.normal(ks[6], (IN_DIM,), dtype=jnp.float32) * 0.01
        return {'feat_in': feat_in, 'adj': adj, 'W': W, 'b': b, 'w_src': w_src, 'w_dst': w_dst, 'H_w': H_w, 'H_b': H_b}
    _L1_gnn_all = _L1_gnn_setup()
    _L1_gnn_in = {k: v for k, v in _L1_gnn_all.items() if k in ('W', 'b', 'w_src', 'w_dst', 'H_w', 'H_b')}
    del _L1_gnn_all
    return {'x': x, 'adj': adj, 'L0_gnn_Wq': _L0_gnn_in['Wq'], 'L0_gnn_bq': _L0_gnn_in['bq'], 'L0_gnn_Wk': _L0_gnn_in['Wk'], 'L0_gnn_bk': _L0_gnn_in['bk'], 'L0_gnn_Wv': _L0_gnn_in['Wv'], 'L0_gnn_bv': _L0_gnn_in['bv'], 'L0_gnn_Wf': _L0_gnn_in['Wf'], 'L0_gnn_bf': _L0_gnn_in['bf'], 'L1_gnn_W': _L1_gnn_in['W'], 'L1_gnn_b': _L1_gnn_in['b'], 'L1_gnn_w_src': _L1_gnn_in['w_src'], 'L1_gnn_w_dst': _L1_gnn_in['w_dst'], 'L1_gnn_H_w': _L1_gnn_in['H_w'], 'L1_gnn_H_b': _L1_gnn_in['H_b']}

def reference(x, adj, L0_gnn_Wq, L0_gnn_bq, L0_gnn_Wk, L0_gnn_bk, L0_gnn_Wv, L0_gnn_bv, L0_gnn_Wf, L0_gnn_bf, L1_gnn_W, L1_gnn_b, L1_gnn_w_src, L1_gnn_w_dst, L1_gnn_H_w, L1_gnn_H_b):
    import jax
    import jax.numpy as jnp

    def _L0_gnn_ref(seq_inputs, Wq, bq, Wk, bk, Wv, bv, Wf, bf, graph_mask):
        import jax, jax.numpy as jnp
        import numpy as np
        B, S, H = (4, 1024, 384)
        NUM_HEADS = 6
        HEAD_SIZE = H // NUM_HEADS
        NEG = -9000000000000000.0

        def _heads(x):
            b, s, _ = x.shape
            return x.reshape(b, s, NUM_HEADS, HEAD_SIZE).transpose(0, 2, 1, 3)
        q = _heads(seq_inputs @ Wq + bq)
        k = _heads(seq_inputs @ Wk + bk)
        v = _heads(seq_inputs @ Wv + bv)
        scores = jnp.einsum('bhqd,bhkd->bhqk', q, k) / np.sqrt(HEAD_SIZE)
        bias = jnp.where(graph_mask, 0.0, NEG)[:, None]
        probs = jax.nn.softmax(scores + bias, axis=-1)
        ctx = jnp.einsum('bhqk,bhkd->bhqd', probs, v)
        ctx = ctx.transpose(0, 2, 1, 3).reshape(seq_inputs.shape[0], seq_inputs.shape[1], H)
        return ctx @ Wf + bf

    def _L1_gnn_ref(feat_in, adj, W, b, w_src, w_dst, H_w, H_b):
        import jax, jax.numpy as jnp
        import numpy as np
        ATT_HEAD = 12
        IN_DIM = 384
        OUT_DIM = IN_DIM // ATT_HEAD
        LEAKY_ALPHA = 0.2
        B, N = (8, 256)
        h = jnp.einsum('bnd,ade->bane', feat_in, W)
        th = jnp.tanh(h)
        attn_src = jnp.einsum('bane,aeo->bano', th, w_src)
        attn_dst = jnp.einsum('bane,aeo->bano', th, w_dst)
        attn = attn_src + jnp.swapaxes(attn_dst, 2, 3)
        attn = jnp.where(attn >= 0, attn, LEAKY_ALPHA * attn)
        mask = ~adj[:, None, :, :]
        attn = jnp.where(mask, jnp.float32(-999.0), attn)
        attn = jax.nn.softmax(attn, axis=-1)
        feat_out = jnp.einsum('banm,bame->bane', attn, h) + b
        feat_out = jnp.swapaxes(feat_out, 1, 2).reshape(feat_in.shape[0], feat_in.shape[1], -1)
        feat_out = jax.nn.elu(feat_out)
        gate = jax.nn.sigmoid(feat_in @ H_w.T + H_b)
        return gate * feat_out + (1.0 - gate) * feat_in
    h = jnp.maximum(_layernorm(x, axis=-1), 0.0)
    x = x + _L0_gnn_ref(h, L0_gnn_Wq, L0_gnn_bq, L0_gnn_Wk, L0_gnn_bk, L0_gnn_Wv, L0_gnn_bv, L0_gnn_Wf, L0_gnn_bf, adj)
    h = jnp.maximum(_layernorm(x, axis=-1), 0.0)
    x = x + _L1_gnn_ref(h, adj, L1_gnn_W, L1_gnn_b, L1_gnn_w_src, L1_gnn_w_dst, L1_gnn_H_w, L1_gnn_H_b)
    return x

_drawn_inputs = setup_inputs


def setup_inputs(seed=0):
    import zlib

    import numpy as np

    out = dict(_drawn_inputs(seed))
    spreads = {'L0_gnn_bq': (0.0, 0.677),
     'L0_gnn_bk': (0.0, 2.0),
     'L0_gnn_bv': (0.0, 0.1),
     'L0_gnn_bf': (0.0, 0.1),
     'L1_gnn_b': (0.0, 0.1)}
    factors = {'L1_gnn_w_src': 12.069, 'L1_gnn_H_b': 37.618}
    for name, (base, spread) in spreads.items():
        noise = np.random.default_rng([zlib.crc32(name.encode()), seed]).standard_normal(out[name].shape)
        drawn = base * np.exp(spread * noise) if base else spread * noise
        out[name] = jnp.asarray(drawn.astype(out[name].dtype))
    for name, factor in factors.items():
        out[name] = (out[name] * factor).astype(out[name].dtype)
    return out
```

```python
from contextlib import ExitStack

import numpy as np

import concourse.bass as bass
from concourse import mybir

F32, F16, BF16, U8 = mybir.dt.float32, mybir.dt.float16, mybir.dt.bfloat16, mybir.dt.uint8
ALU = mybir.AluOpType
ACT = mybir.ActivationFunctionType
AX_X = mybir.AxisListType.X
RMAX = bass.bass_isa.ReduceOp.max

P = 128
T = 256
H = 384
NT = T // P
NC = H // P
H0, D0 = 6, 64
H1, D1 = 12, 32
BIG = 9.0e15
ALPHA = 0.2
EPS = 1e-5
XS = 1024.0
WS = 16384.0
VS = 2.0 ** -17
WQ, WK, WV, WF, WH, WG = range(6)
TERMS = ((0, 0), (0, 1), (1, 0))



def order_of_steps():
    units = [("A", u) for u in range(6)] + [("B", u) for u in range(12)]
    fill = {
        0: [("C", "RECIP1", 0), ("C", "OUT_T", 0), ("P", "LOAD", 0)],
        1: [("C", "OUT_T", 1), ("A", "RES_ROW", 0)],
        2: [("C", "ELU_MIN", 0), ("P", "STATS0", 0), ("P", "RSTD0", 0)],
        3: [("C", "ELU_EXP", 0), ("P", "NORM0", 0), ("P", "LN_T0", 0)],
        4: [("P", "LN_T0", 1), ("C", "FINISH", 0), ("C", "STORE", 0)],
        6: [("P", "QK", 0)],
        7: [("P", "QK", 1)],
        8: [("P", "QK", 2)],
        9: [("A", "OUT0", 0), ("A", "OUT0", 1), ("A", "STATS1", 0), ("A", "RSTD1", 0)],
        10: [("P", "V", 0), ("A", "NORM1", 0)],
        11: [("A", "LN_T1", 0), ("A", "LN_T1", 1), ("P", "V", 1)],
        12: [("A", "HEADS", 0)],
        13: [("A", "HEADS", 1), ("A", "SCORE_PROD", 0)],
        14: [("A", "GATE", 0)],
        15: [("A", "GATE", 1), ("A", "GATE_TANH", 0), ("A", "SCORE_SUM", 0)],
        16: [("A", "SKIP", 0)],
        17: [("A", "DST_T", 0)],
        18: [("P", "MASK", 0)],
    }
    steps = []
    n = len(units)
    for i in range(n + 3):
        if 0 <= i - 3 < n:
            ph, u = units[i - 3]
            if ph == "A":
                steps.append(("A", "PT0", u))
                if u % 2 == 1:
                    steps.append(("A", "PV0", u // 2))
            else:
                steps.append(("B", "PT1", u))
                if u % 4 == 3:
                    steps.append(("B", "PV1", u // 4))
        if i + 1 < n and units[i + 1][0] == "B" and units[i + 1][1] % 2 == 0:
            steps.append(("B", "DST", units[i + 1][1] // 2))
        if 0 <= i - 1 < n:
            ph, u = units[i - 1]
            steps.append((ph, "EXP0" if ph == "A" else "EXP1", u))
            if ph == "A":
                steps.append(("A", "NORMP0", u))
        if i < n:
            ph, u = units[i]
            steps.append((ph, "QK0" if ph == "A" else "LEAKY1", u))
        steps += fill.get(i, [])
    return steps


ORDER = order_of_steps()
LAG = {"P": -1, "A": 0, "B": 1, "C": 2}


class It:

    def __init__(self, ref, reg=None):
        self.ref, self.reg = ref, reg

    def back(self, k):
        return It(self.ref - k, self.reg)

    def batch(self, phase):
        return self.ref - LAG[phase]

    def batch_value(self, phase):
        b = self.batch(phase)
        return b if self.reg is None else self.reg * 2 + b


class Count:

    def __init__(self, n_batch, per_step, unit=1):
        self.per_step, self.unit, self.n = per_step, unit, n_batch
        self.starts = {-1: 0}
        for it in range(-1, n_batch + 2):
            self.starts[it + 1] = self.starts[it] + sum(per_step[s] for ph, s, _ in ORDER if self._on(ph, it, s))
        self.per = self.starts[3] - self.starts[2]

    def _on(self, phase, it, step):
        return step in self.per_step and 0 <= it - LAG[phase] < self.n

    def _value(self, it, inside):
        v = (self.starts[it.ref] + inside) * self.unit
        return v if it.reg is None else it.reg * (2 * self.per * self.unit) + v

    def _before(self, it, step, idx):
        n = 0
        for ph, s, i in ORDER:
            if (s, i) == (step, idx):
                assert 0 <= it.ref - LAG[ph] < self.n, (step, it.ref)
                return n
            if self._on(ph, it.ref, s):
                n += self.per_step[s]
        raise KeyError((step, idx))

    def before(self, it, step, idx=0, less=0):
        return self._value(it, self._before(it, step, idx) - less)

    def some_before(self, it, step, idx=0, less=0):
        return self.starts[it.ref] + self._before(it, step, idx) - less > 0

    def after(self, it, step, idx=0, k=None):
        return self._value(it, self._before(it, step, idx) + (self.per_step[step] if k is None else k))


def build(nc, x, adj, w_all, bq, bk, bv, bf, gat_b, w_src, w_dst, gate_b, out):
    NB = x.shape[0]
    LOOP = (NB - 4) // 2
    assert NB % 2 == 0 and LOOP >= 1

    x_v = x.rearrange("b (t p) h -> b p t h", p=P)
    out_v = out.rearrange("b (t p) h -> b p t h", p=P)
    adj_v = adj.rearrange("b (t p) m -> b p t m", p=P)
    w_v = w_all.rearrange("w (c p) n -> w p c n", p=P)

    with ExitStack() as ctx:
        def sb(name, shape, dt=F32):
            return ctx.enter_context(nc.sbuf_tensor(name, shape, dt))

        def sem(name):
            return ctx.enter_context(nc.semaphore(name))

        bank0 = ctx.enter_context(nc.psum_tensor("bank0", [P, 512], F32))
        bank1 = ctx.enter_context(nc.psum_tensor("bank1", [P, 512], F32))
        score0 = [ctx.enter_context(nc.psum_tensor(f"score0_{i}", [P, 512], F32)) for i in range(2)]
        dst_ps = [ctx.enter_context(nc.psum_tensor(f"dst_ps{i}", [P, 512], F32)) for i in range(2)]
        pt0_ps = ctx.enter_context(nc.psum_tensor("pt0_ps", [P, 512], F32))
        pt1_ps = ctx.enter_context(nc.psum_tensor("pt1_ps", [P, 512], F32))

        w16 = sb("w16", [P, 6, 2, NC, H], F16)
        wmax = sb("wmax", [P, 6])
        wmax_all = sb("wmax_all", [P, 6])
        wscale = sb("wscale", [P, 6])
        post = sb("post", [P, 6])
        post_q = sb("post_q", [P, 1])
        post_f = sb("post_f", [P, 1])
        bq_c = sb("bq_c", [P, NC])
        bk_c = sb("bk_c", [P, NC])
        bv_c = sb("bv_c", [P, NC])
        bv_w = sb("bv_w", [P, NC, P])
        out0_row = sb("out0_row", [P, H])
        gat_b_row = sb("gat_b_row", [P, D1])
        gate_b_row = sb("gate_b_row", [P, H])
        src_row = sb("src_row", [P, H])
        dst_row = sb("dst_row", [P, H])
        ident = sb("ident", [P, P])
        ident_b = sb("ident_b", [P, P], BF16)
        pick = sb("pick", [P, H1, P], BF16)
        half = sb("half", [P, NT])

        xb = [sb(f"xb{i}", [P, NT, H]) for i in range(2)]
        adj_raw = [sb(f"adj_raw{i}", [P, NT, T], U8) for i in range(2)]
        mask = [sb(f"mask{i}", [P, NT, T]) for i in range(2)]
        bn = sb("bn", [P, NT, 6])
        mv = [sb(f"mv{i}", [P, NT, 2]) for i in range(2)]
        veps = sb("veps", [P, 2, NT])
        rstd = [sb(f"rstd{i}", [P, NT]) for i in range(2)]
        xn = [sb(f"xn{i}", [P, NT, H]) for i in range(2)]
        h16 = [sb(f"h16_{i}", [P, 2, NC, T], F16) for i in range(2)]
        qT = [sb(f"qT{i}", [P, 3, T]) for i in range(2)]
        kz = [sb(f"kz{i}", [P, H0, T]) for i in range(2)]
        vv = [sb(f"vv{i}", [P, NT, H]) for i in range(2)]
        y0 = sb("y0", [P, 2, 2, T])
        p0 = sb("p0", [P, 3, 2, T])
        min0 = sb("min0", [P, 6, 2])
        sum0 = sb("sum0", [P, 6, 2])
        rec0 = sb("rec0", [P, 6, 2])
        pT0 = sb("pT0", [P, 2, 2, NT, T])
        c16 = sb("c16", [P, 2, 3, T], F16)
        xc = sb("xc", [P, NT, H])
        x2 = sb("x2", [P, NT, H])
        th = sb("th", [P, NT, H])
        prod = sb("prod", [P, 2, NT, H])
        hv = [sb(f"hv{i}", [P, NT, H]) for i in range(2)]
        s8 = [sb(f"s8_{i}", [P, NT, H1]) for i in range(2)]
        nd = sb("nd", [P, NT, H1])
        nd_r = sb("nd_r", [P, NT, H1])
        nd_parts = sb("nd_parts", [P, NT, 3, H1], BF16)
        ndT = [sb(f"ndT{i}", [P, T], BF16) for i in range(2)]
        gpre = sb("gpre", [P, NT, H])
        gate = [sb(f"gate{i}", [P, NT, H]) for i in range(2)]
        hskip = [sb(f"hskip{i}", [P, NT, H]) for i in range(2)]
        xskip = [sb(f"xskip{i}", [P, NT, H]) for i in range(2)]
        dst5 = sb("dst5", [P, 2, 2, T])
        yw = sb("yw", [P, 2, 2, T])
        y1 = sb("y1", [P, 2, 2, T])
        p1 = sb("p1", [P, 3, 2, T])
        min1 = sb("min1", [P, 12, 2])
        sum1 = sb("sum1", [P, NT, H1])
        rec1 = sb("rec1", [P, NT, H1])
        pT1 = sb("pT1", [P, 2, 4, NT, T])
        setup_room = pT1[:].rearrange("p a q k t -> p (a q k t)")
        wstage = setup_room[:, 0:2 * NC * H].rearrange("p (w c n) -> p w c n", w=2, c=NC)
        wabs = setup_room[:, 2 * NC * H:3 * NC * H].rearrange("p (c n) -> p c n", c=NC)
        oT = sb("oT", [P, 3, T])
        o1 = sb("o1", [P, NT, H])
        o1m = sb("o1m", [P, NT, H])
        ya = sb("ya", [P, NT, H])
        yb = sb("yb", [P, NT, H])

        s_w = [sem(f"s_weight{i}") for i in range(6)]
        s_small = sem("s_small_inputs")
        s_wmax = sem("s_wmax")
        s_wmax_all = sem("s_wmax_all")
        s_w16 = sem("s_w16")
        s_setup = sem("s_setup_dve")
        s_setup_act = sem("s_setup_act")
        s_pool_const = sem("s_pool_const")
        s_bvw = sem("s_bvw")
        s_row = sem("s_row")
        s_rowdone = sem("s_rowdone")

        s_x = [sem(f"s_x_loaded{i}") for i in range(2)]
        s_adj = [sem(f"s_adj_loaded{i}") for i in range(2)]
        s_mask, n_mask = sem("s_mask"), Count(NB, {"MASK": 1})
        s_bn, n_bn = sem("s_bn_stats"), Count(NB, {"STATS0": 1, "STATS1": 1})
        s_mv, n_mv = sem("s_mean_var"), Count(NB, {"STATS0": 1, "STATS1": 1})
        s_veps, n_veps = sem("s_veps"), Count(NB, {"RSTD0": 1, "RSTD1": 1})
        s_rstd, n_rstd = sem("s_rstd"), Count(NB, {"RSTD0": 1, "RSTD1": 1})
        s_norm, n_norm = sem("s_normalised"), Count(NB, {"NORM0": 1, "NORM1": 1})
        jobs0 = {"LN_T0": 1, "QK": 1, "V": 1, "PV0": 1, "OUT0": 1}
        s_b0_full, n_b0 = sem("s_bank0_full"), Count(NB, jobs0)
        s_b0_done = sem("s_bank0_done")
        jobs1 = {"LN_T1": 1, "HEADS": 1, "GATE": 1, "DST_T": 1, "PV1": 1, "OUT_T": 1}
        s_b1_full, n_b1 = sem("s_bank1_full"), Count(NB, jobs1)
        s_b1_done = sem("s_bank1_done")
        s_hi0, n_hi0 = sem("s_high_part0"), Count(NB, {"LN_T0": 1, "PV0": 1})
        s_hi1, n_hi1 = sem("s_high_part1"), Count(NB, {"LN_T1": 1})
        s_s0, n_s0 = sem("s_scores0"), Count(NB, {"QK0": 1})
        s_y0 = sem("s_masked0")
        s_e0, n_e0 = sem("s_exp0"), Count(NB, {"EXP0": 1})
        s_rec0, n_np0 = sem("s_reciprocal0"), Count(NB, {"NORMP0": 1})
        s_p0 = sem("s_probs0")
        s_t0, n_t0 = sem("s_probs0_transposed"), Count(NB, {"PT0": 1})
        s_pT0 = sem("s_pT0_in_sbuf")
        s_xc, n_xc = sem("s_residual_row"), Count(NB, {"RES_ROW": 1})
        s_th, n_th = sem("s_tanh_heads"), Count(NB, {"HEADS": 1})
        s_prod, n_prod = sem("s_score_products"), Count(NB, {"SCORE_PROD": 1})
        s_sd, n_sd = sem("s_score_parts"), Count(NB, {"SCORE_SUM": 5})
        s_nd, n_nd = sem("s_dst_middle_part"), Count(NB, {"SCORE_SUM": 1})
        s_gtanh, n_gtanh = sem("s_gate"), Count(NB, {"GATE_TANH": 1})
        s_skip, n_skip = sem("s_skip"), Count(NB, {"SKIP": 2})
        s_db, n_db = sem("s_dst_rows"), Count(NB, {"DST": 1})
        s_d5 = sem("s_dst_rows_scaled")
        s_lk, n_lk = sem("s_leaky"), Count(NB, {"LEAKY1": 2})
        s_y1, n_y1 = sem("s_masked1"), Count(NB, {"LEAKY1": 1})
        s_e1, n_e1 = sem("s_exp1"), Count(NB, {"EXP1": 1})
        s_t1, n_t1 = sem("s_probs1_transposed"), Count(NB, {"PT1": 1})
        s_pT1 = sem("s_pT1_in_sbuf")
        s_rec1, n_rec1 = sem("s_reciprocal1"), Count(NB, {"RECIP1": 1})
        s_om, n_om = sem("s_elu_min"), Count(NB, {"ELU_MIN": 2})
        s_oe, n_oe = sem("s_elu_exp"), Count(NB, {"ELU_EXP": 1})
        s_fin, n_fin = sem("s_finish"), Count(NB, {"FINISH": 4})
        s_out, n_out = sem("s_stored"), Count(NB, {"STORE": 1}, 16)

        def ready(eng, value):
            if isinstance(value, int):
                return value
            if eng.engine not in count_regs:
                count_regs[eng.engine] = [eng.alloc_register(f"count{i}_{eng.engine.name}") for i in range(3)]
            regs = count_regs[eng.engine]
            regs.append(regs.pop(0))
            eng.reg_mov(regs[-1], value)
            return regs[-1]

        count_regs = {}

        def loaded(it, phase):
            v = 16 * (it.batch(phase) // 2 + 1)
            return v if it.reg is None else it.reg * 16 + v

        def walk(eng, parts):
            def iteration(it):
                for phase, step, idx in ORDER:
                    if step in parts and 0 <= it.batch(phase) < NB:
                        parts[step](it, it.batch(phase) % 2, idx)
            for n in range(-1, 2):
                iteration(It(n))
            with eng.Fori(0, LOOP) as j:
                iteration(It(2, j))
                iteration(It(3, j))
            for n in range(NB - 2, NB + 2):
                iteration(It(n))

        block = ctx.enter_context(nc.Block())

        @block.sync
        def _(sp):
            small = [
                (bq_c[:], bq), (bk_c[:], bk),
                (bv_c[:], bv),
                (out0_row[:], bf.partition_broadcast(P)), (gat_b_row[:], gat_b.partition_broadcast(P)),
                (gate_b_row[:], gate_b.partition_broadcast(P)), (src_row[:], w_src.partition_broadcast(P)),
                (dst_row[:], w_dst.partition_broadcast(P)),
            ]
            for w in range(2):
                sp.dma_start(wstage[:, w], w_v[w]).then_inc(s_w[w], 16)
            for dst, src in small:
                sp.dma_start(dst, src).then_inc(s_small, 16)
            for w in range(2, 6):
                sp.wait_ge(s_w16, w - 1)
                sp.dma_start(wstage[:, w % 2], w_v[w]).then_inc(s_w[w], 16)

            def load(it, par, _):
                if it.batch("P") >= 2:
                    old = it.back(2)
                    sp.wait_ge(s_norm, n_norm.after(old, "NORM0"))
                    sp.wait_ge(s_xc, n_xc.after(it.back(1), "RES_ROW"))
                    sp.wait_ge(s_mask, n_mask.after(old, "MASK"))
                b = it.batch_value("P")
                src_x = x_v[b] if it.reg is None else x_v[bass.ds(b, 1)].rearrange("a p t h -> (a p) t h")
                src_a = adj_v[b] if it.reg is None else adj_v[bass.ds(b, 1)].rearrange("a p t m -> (a p) t m")
                sp.dma_start(xb[par][:], src_x).then_inc(s_x[par], 16)
                sp.dma_start(adj_raw[par][:], src_a).then_inc(s_adj[par], 16)

            def store(it, par, _):
                sp.wait_ge(s_fin, n_fin.after(it, "FINISH"))
                b = it.batch_value("C")
                dst = out_v[b] if it.reg is None else out_v[bass.ds(b, 1)].rearrange("a p t h -> (a p) t h")
                sp.dma_start(dst, yb[:]).then_inc(s_out, 16)

            walk(sp, {"LOAD": load, "STORE": store})
            sp.wait_ge(s_out, 16 * NB)

        @block.tensor
        def _(pe):
            mm = nc.tensor.matmul

            pe.wait_ge(s_w[WF], 16)
            pe.wait_ge(s_bvw, 1)
            for c in range(NC):
                last = mm(bank0[:, 0:H], bv_w[:, c, :], wstage[:, WF % 2, c, :], start=c == 0, stop=c == NC - 1)
            last.then_inc(s_row, 1)
            pe.wait_ge(s_rowdone, 1)
            pe.wait_ge(s_pool_const, 8)
            pe.wait_ge(s_w16, 6)

            def bank0_free(it, step, idx):
                if n_b0.some_before(it, step, idx):
                    pe.wait_ge(s_b0_done, n_b0.before(it, step, idx))

            def bank1_free(it, step, idx):
                if n_b1.some_before(it, step, idx):
                    pe.wait_ge(s_b1_done, n_b1.before(it, step, idx))

            def transpose_norm(bank, src, k):
                for i, c in enumerate((0, 1) if k == 0 else (2,)):
                    for t in range(NT):
                        last = nc.tensor.transpose(bank[:, i * T + t * P:i * T + (t + 1) * P],
                                                   src[:, t, c * P:(c + 1) * P], ident[:])
                return last

            def to_rows(bank, act, t, w):
                n = 0
                for c in range(NC):
                    for a, b in TERMS:
                        last = mm(bank[:, 0:H], act[:, a, c, t * P:(t + 1) * P], w16[:, w, b, c, :],
                                  start=n == 0, stop=n == 3 * NC - 1)
                        n += 1
                return last

            def ln_t0(it, par, k):
                if k == 0:
                    pe.wait_ge(s_norm, n_norm.after(it, "NORM0"))
                bank0_free(it, "LN_T0", k)
                transpose_norm(bank0, xn[0], k).then_inc(s_b0_full, 1)

            def qk(it, par, p):
                if p == 0:
                    pe.wait_ge(s_b0_done, n_b0.after(it, "LN_T0", 1))
                bank0_free(it, "QK", p)
                for i, w in enumerate((WQ, WK)):
                    n = 0
                    for c in range(NC):
                        for a, b in TERMS:
                            last = mm(bank0[:, i * T:(i + 1) * T], w16[:, w, a, c, p * P:(p + 1) * P],
                                      h16[0][:, b, c, :], start=n == 0, stop=n == 3 * NC - 1)
                            n += 1
                last.then_inc(s_b0_full, 1)

            def v(it, par, t):
                bank0_free(it, "V", t)
                to_rows(bank0, h16[0], t, WV).then_inc(s_b0_full, 1)

            def qk0(it, par, u):
                p, qt = divmod(u, 2)
                if u == 0:
                    pe.wait_ge(s_b0_done, n_b0.after(it.back(1), "V", 1))
                if n_s0.some_before(it, "QK0", u, 1):
                    pe.wait_ge(s_y0, n_s0.before(it, "QK0", u, 1))
                mm(score0[u % 2][:], qT[par][:, p, qt * P:(qt + 1) * P], kz[par][:, 2 * p:2 * p + 2, :],
                   start=True, stop=True).then_inc(s_s0, 1)

            def pt0(it, par, u):
                pe.wait_ge(s_p0, n_np0.after(it, "NORMP0", u))
                if n_t0.some_before(it, "PT0", u):
                    pe.wait_ge(s_pT0, n_t0.before(it, "PT0", u))
                for hh in range(2):
                    for kt in range(NT):
                        last = nc.tensor.transpose(pt0_ps[:, (2 * hh + kt) * P:(2 * hh + kt + 1) * P],
                                                   p0[:, u % 3, hh, kt * P:(kt + 1) * P], ident[:])
                last.then_inc(s_t0, 1)

            def pv0(it, par, p):
                pe.wait_ge(s_pT0, n_t0.after(it, "PT0", 2 * p + 1))
                bank0_free(it, "PV0", p)
                for kt in range(NT):
                    for hh in range(2):
                        h = 2 * p + hh
                        last = mm(bank0[D0 * hh:D0 * (hh + 1), 0:T], vv[par][:, kt, h * D0:(h + 1) * D0],
                                  pT0[:, p % 2, hh, kt, :], start=kt == 0, stop=kt == NT - 1)
                last.then_inc(s_b0_full, 1)

            def out0(it, par, t):
                bank0_free(it, "OUT0", t)
                to_rows(bank0, c16, t, WF).then_inc(s_b0_full, 1)

            def ln_t1(it, par, k):
                if k == 0:
                    pe.wait_ge(s_norm, n_norm.after(it, "NORM1"))
                bank1_free(it, "LN_T1", k)
                transpose_norm(bank1, xn[1], k).then_inc(s_b1_full, 1)

            def heads(it, par, t):
                bank1_free(it, "HEADS", t)
                to_rows(bank1, h16[1], t, WH).then_inc(s_b1_full, 1)

            def gate_proj(it, par, t):
                bank1_free(it, "GATE", t)
                to_rows(bank1, h16[1], t, WG).then_inc(s_b1_full, 1)

            def dst_t(it, par, _):
                parts, free = ready(pe, n_sd.after(it, "SCORE_SUM")), ready(pe, n_b1.before(it, "DST_T"))
                pe.wait_ge(s_pool_const, 8)
                pe.wait_ge(s_sd, parts)
                pe.wait_ge(s_b1_done, free)
                view = bank1[:].bitcast(BF16)
                for t in range(NT):
                    last = nc.tensor.transpose(view[0:3 * H1, t * P:(t + 1) * P],
                                               nd_parts[:, t].rearrange("p a h -> p (a h)"), ident_b[:])
                last.then_inc(s_b1_full, 1)

            def dst(it, par, c):
                if c == 0:
                    pe.wait_ge(s_b1_done, n_b1.after(it.back(1), "DST_T"))
                if n_y1.some_before(it, "LEAKY1", 2 * c, 2):
                    pe.wait_ge(s_y1, n_y1.before(it, "LEAKY1", 2 * c, 2))
                for hh in range(2):
                    last = mm(dst_ps[c % 2][:, hh * T:(hh + 1) * T], pick[:, 2 * c + hh, :], ndT[par][:],
                              start=True, stop=True)
                last.then_inc(s_db, 1)

            def pt1(it, par, u):
                pe.wait_ge(s_e1, n_e1.after(it, "EXP1", u))
                if n_t1.some_before(it, "PT1", u):
                    pe.wait_ge(s_pT1, n_t1.before(it, "PT1", u))
                for hh in range(2):
                    for kt in range(NT):
                        last = nc.tensor.transpose(pt1_ps[:, (2 * hh + kt) * P:(2 * hh + kt + 1) * P],
                                                   p1[:, u % 3, hh, kt * P:(kt + 1) * P], ident[:])
                last.then_inc(s_t1, 1)

            def pv1(it, par, g):
                pe.wait_ge(s_pT1, n_t1.after(it, "PT1", 4 * g + 3))
                bank1_free(it, "PV1", g)
                for kt in range(NT):
                    for q in range(4):
                        h = 4 * g + q
                        last = mm(bank1[D1 * q:D1 * (q + 1), 0:T], hv[par][:, kt, h * D1:(h + 1) * D1],
                                  pT1[:, g % 2, q, kt, :], start=kt == 0, stop=kt == NT - 1,
                                  tile_position=(0, D1 * q))
                last.then_inc(s_b1_full, 1)

            def out_t(it, par, t):
                if t == 0:
                    pe.wait_ge(s_b1_done, n_b1.after(it.back(1), "PV1", 2))
                bank1_free(it, "OUT_T", t)
                for g in range(3):
                    last = nc.tensor.transpose(bank1[:, g * P:(g + 1) * P], oT[:, g, t * P:(t + 1) * P], ident[:])
                last.then_inc(s_b1_full, 1)

            walk(pe, {"LN_T0": ln_t0, "QK": qk, "V": v, "QK0": qk0, "PT0": pt0, "PV0": pv0, "OUT0": out0,
                      "LN_T1": ln_t1, "HEADS": heads, "GATE": gate_proj, "DST_T": dst_t, "DST": dst,
                      "PT1": pt1, "PV1": pv1, "OUT_T": out_t})

        @block.scalar
        def _(act):
            op = nc.scalar.activation

            act.wait_ge(s_wmax_all, 1)
            act.wait_ge(s_setup, SETUP_SCALES)

            def chunks(k):
                return slice(0, 2) if k == 0 else slice(2, 3)

            def ln_t0(it, par, k):
                act.wait_ge(s_b0_full, n_b0.after(it, "LN_T0", k))
                c = chunks(k)
                n = (c.stop - c.start) * T
                op(h16[0][:, 0, c, :], bank0[:, 0:n].rearrange("p (c t) -> p c t", t=T), ACT.Relu).then_inc(s_hi0, 1)

            def ln_t1(it, par, k):
                act.wait_ge(s_b1_full, n_b1.after(it, "LN_T1", k))
                c = chunks(k)
                n = (c.stop - c.start) * T
                op(h16[1][:, 0, c, :], bank1[:, 0:n].rearrange("p (c t) -> p c t", t=T), ACT.Relu).then_inc(s_hi1, 1)

            def v(it, par, t):
                act.wait_ge(s_b0_full, n_b0.after(it, "V", t))
                op(vv[par][:, t, :], bank0[:, 0:H], ACT.Copy, scale=VS).then_inc(s_b0_done, 1)

            def exp0(it, par, u):
                act.wait_ge(s_y0, n_s0.after(it, "QK0", u))
                if n_t0.some_before(it, "PT0", u, 2):
                    act.wait_ge(s_t0, n_t0.before(it, "PT0", u, 2))
                for hh in range(2):
                    last = op(p0[:, u % 3, hh, :], y0[:, u % 2, hh, :], ACT.Exp, bias=min0[:, u, hh:hh + 1],
                              scale=-1.0, accum_out=sum0[:, u, hh:hh + 1])
                last.then_inc(s_e0, 1)

            def pt0(it, par, u):
                p, qt = divmod(u, 2)
                act.wait_ge(s_t0, n_t0.after(it, "PT0", u))
                op(pT0[:, p % 2, :, :, qt * P:(qt + 1) * P],
                   pt0_ps[:].rearrange("p (h k q) -> p h k q", h=2, k=NT), ACT.Copy).then_inc(s_pT0, 1)

            def pv0(it, par, p):
                act.wait_ge(s_b0_full, n_b0.after(it, "PV0", p))
                op(c16[:, 0, p, :], bank0[:, 0:T], ACT.Copy).then_inc(s_hi0, 1)

            def heads(it, par, t):
                act.wait_ge(s_b1_full, n_b1.after(it, "HEADS", t))
                if t == 0 and it.batch("A") >= 1:
                    act.wait_ge(s_prod, n_prod.after(it.back(1), "SCORE_PROD"))
                op(th[:, t, :], bank1[:, 0:H], ACT.Tanh, scale=post[:, WH:WH + 1]).then_inc(s_th, 1)
                op(hv[par][:, t, :], bank1[:, 0:H], ACT.Copy, scale=post[:, WH:WH + 1]).then_inc(s_b1_done, 1)

            def gate_tanh(it, par, _):
                act.wait_ge(s_b1_done, n_b1.after(it, "GATE", 1))
                op(gate[par][:], gpre[:], ACT.Tanh, scale=0.5).then_inc(s_gtanh, 1)

            def dst(it, par, c):
                act.wait_ge(s_db, n_db.after(it, "DST", c))
                if n_y1.some_before(it, "LEAKY1", 2 * c, 2):
                    act.wait_ge(s_y1, n_y1.before(it, "LEAKY1", 2 * c, 2))
                op(dst5[:, c % 2].rearrange("p h t -> p (h t)"), dst_ps[c % 2][:], ACT.Copy, scale=ALPHA).then_inc(s_d5, 1)

            def exp1(it, par, u):
                c, t = divmod(u, 2)
                act.wait_ge(s_y1, n_y1.after(it, "LEAKY1", u))
                if n_t1.some_before(it, "PT1", u, 2):
                    act.wait_ge(s_t1, n_t1.before(it, "PT1", u, 2))
                if u == 0 and it.batch("B") >= 1:
                    act.wait_ge(s_rec1, n_rec1.after(it, "RECIP1"))
                for hh in range(2):
                    h = 2 * c + hh
                    last = op(p1[:, u % 3, hh, :], y1[:, u % 2, hh, :], ACT.Exp, bias=min1[:, u, hh:hh + 1],
                              scale=-1.0, accum_out=sum1[:, t, h:h + 1])
                last.then_inc(s_e1, 1)

            def pt1(it, par, u):
                c, t = divmod(u, 2)
                g, q = divmod(2 * c, 4)
                act.wait_ge(s_t1, n_t1.after(it, "PT1", u))
                op(pT1[:, g % 2, q:q + 2, :, t * P:(t + 1) * P],
                   pt1_ps[:].rearrange("p (h k q) -> p h k q", h=2, k=NT), ACT.Copy).then_inc(s_pT1, 1)

            def pv1(it, par, g):
                act.wait_ge(s_b1_full, n_b1.after(it, "PV1", g))
                op(oT[:, g, :], bank1[:, 0:T], ACT.Copy).then_inc(s_b1_done, 1)

            def elu_exp(it, par, _):
                act.wait_ge(s_om, n_om.after(it, "ELU_MIN"))
                op(o1m[:], o1m[:], ACT.Exp).then_inc(s_oe, 1)

            walk(act, {"LN_T0": ln_t0, "V": v, "EXP0": exp0, "PT0": pt0, "PV0": pv0, "LN_T1": ln_t1,
                       "HEADS": heads, "GATE_TANH": gate_tanh, "DST": dst, "EXP1": exp1, "PT1": pt1,
                       "PV1": pv1, "ELU_EXP": elu_exp})

        @block.vector
        def _(dve):
            chain = [0]

            def own(ins):
                chain[0] += 1
                ins.then_inc(s_setup, 1)
                dve.wait_ge(s_setup, chain[0])

            V = nc.vector
            dve.wait_ge(s_small, 16 * 8)
            for c in range(NC):
                last = V.tensor_copy(bv_w[:, c, :], bv_c[:, c:c + 1].broadcast_to([P, P]))
            last.then_inc(s_bvw, 1)
            own(V.tensor_scalar(bq_c[:], bq_c[:], -1.0 / 8.0, None, ALU.mult))
            own(V.tensor_scalar(src_row[:], src_row[:], -(1.0 - ALPHA), None, ALU.mult))
            own(V.tensor_scalar(dst_row[:], dst_row[:], -1.0, None, ALU.mult))
            for w in range(6):
                dve.wait_ge(s_w[w], 16)
                st = wstage[:, w % 2]
                own(V.scalar_tensor_tensor(wabs, st, -1.0, st, ALU.mult, ALU.max))
                own(V.reduce_max(wmax[:, w:w + 1], wabs.rearrange("p c n -> p (c n)"), AX_X))
                V.tensor_scalar(wmax[:, w:w + 1], wmax[:, w:w + 1], 1e-30, None, ALU.max).then_inc(s_wmax, 1)
                dve.wait_ge(s_wmax_all, w + 1)
                own(V.reciprocal(wscale[:, w:w + 1], wmax_all[:, w:w + 1]))
                own(V.tensor_scalar(wscale[:, w:w + 1], wscale[:, w:w + 1], WS, None, ALU.mult))
                own(V.reciprocal(post[:, w:w + 1], wscale[:, w:w + 1]))
                own(V.tensor_scalar(w16[:, w, 0], st, wscale[:, w:w + 1], None, ALU.mult))
                if w == WF:
                    dve.wait_ge(s_row, 1)
                    V.tensor_tensor(out0_row[:], bank0[:, 0:H], out0_row[:], ALU.add).then_inc(s_rowdone, 1)
                V.scalar_tensor_tensor(w16[:, w, 1], st, wscale[:, w:w + 1], w16[:, w, 0],
                                       ALU.mult, ALU.subtract).then_inc(s_w16, 1)
            own(V.tensor_tensor(post_f[:], post[:, WV:WV + 1], post[:, WF:WF + 1], ALU.mult))
            own(V.tensor_scalar(post_f[:], post_f[:], 1.0 / (XS * VS), None, ALU.mult))
            own(V.tensor_scalar(post[:], post[:], 1.0 / XS, None, ALU.mult))
            own(V.tensor_scalar(post_q[:], post[:, WQ:WQ + 1], -1.0 / 8.0, None, ALU.mult))
            assert chain[0] == SETUP_SCALES

            def stats(src, k, step):
                def part(it, par, _):
                    if k == 0:
                        dve.wait_ge(s_x[par], loaded(it, "P"))
                    else:
                        dve.wait_ge(s_b0_done, n_b0.after(it, "OUT0", 1))
                    for t in range(NT):
                        last = V.bn_stats(bn[:, t, :], (xb[par] if k == 0 else x2)[:, t, :])
                    last.then_inc(s_bn, 1)
                    written = ready(dve, n_bn.after(it, step))
                    dve.wait_ge(s_pool_const, 8)
                    dve.wait_ge(s_bn, written)
                    for t in range(NT):
                        last = V.bn_aggr(mv[k][:, t, :], bn[:, t, :])
                    last.then_inc(s_mv, 1)
                return part

            def norm(src, k, step, rstep):
                def part(it, par, _):
                    dve.wait_ge(s_rstd, n_rstd.after(it, rstep))
                    for t in range(NT):
                        last = V.tensor_scalar(xn[k][:, t, :], (xb[par] if k == 0 else x2)[:, t, :],
                                               mv[k][:, t, 0:1], rstd[k][:, t:t + 1], ALU.subtract, ALU.mult)
                    last.then_inc(s_norm, 1)
                return part

            def low_part(bank, h, k, relu, s_done):
                c = slice(0, 2) if k == 0 else slice(2, 3)
                n = (c.stop - c.start) * T
                V.scalar_tensor_tensor(h[:, 1, c, :].rearrange("p c t -> p (c t)"), bank[:, 0:n], 0.0,
                                       h[:, 0, c, :].rearrange("p c t -> p (c t)"),
                                       ALU.max, ALU.subtract).then_inc(s_done, 1)

            def ln_t0(it, par, k):
                dve.wait_ge(s_hi0, n_hi0.after(it, "LN_T0", k))
                low_part(bank0, h16[0], k, True, s_b0_done)

            def ln_t1(it, par, k):
                dve.wait_ge(s_hi1, n_hi1.after(it, "LN_T1", k))
                low_part(bank1, h16[1], k, True, s_b1_done)

            def qk(it, par, p):
                dve.wait_ge(s_b0_full, n_b0.after(it, "QK", p))
                V.tensor_scalar(qT[par][:, p, :], bank0[:, 0:T], post_q[:], bq_c[:, p:p + 1], ALU.mult, ALU.add)
                for hh in range(2):
                    r = slice(D0 * hh, D0 * (hh + 1))
                    last = V.tensor_scalar(kz[par][r, 2 * p + hh, :], bank0[r, T:2 * T], post[r, WK:WK + 1],
                                           bk_c[r, p:p + 1], ALU.mult, ALU.add)
                last.then_inc(s_b0_done, 1)

            def qk0(it, par, u):
                qt = u % 2
                masks = ready(dve, n_mask.after(it.back(1), "MASK"))
                scores = ready(dve, n_s0.after(it, "QK0", u))
                used = ready(dve, n_e0.before(it, "EXP0", u, 1))
                dve.wait_ge(s_pool_const, 8)
                if u == 0:
                    dve.wait_ge(s_mask, masks)
                dve.wait_ge(s_s0, scores)
                if n_e0.some_before(it, "EXP0", u, 1):
                    dve.wait_ge(s_e0, used)
                for hh in range(2):
                    last = V.tensor_tensor_reduce(y0[:, u % 2, hh, :], score0[u % 2][:, hh * T:(hh + 1) * T],
                                                  mask[par][:, qt, :], 1.0, 3.0e38, ALU.add, ALU.min,
                                                  min0[:, u, hh:hh + 1])
                last.then_inc(s_y0, 1)

            def normp0(it, par, u):
                dve.wait_ge(s_e0, n_e0.after(it, "EXP0", u))
                V.reciprocal(rec0[:, u, :], sum0[:, u, :]).then_inc(s_rec0, 1)

            def pv0(it, par, p):
                dve.wait_ge(s_hi0, n_hi0.after(it, "PV0", p))
                V.tensor_tensor(c16[:, 1, p, :], bank0[:, 0:T], c16[:, 0, p, :], ALU.subtract).then_inc(s_b0_done, 1)

            def out0(it, par, t):
                dve.wait_ge(s_b0_full, n_b0.after(it, "OUT0", t))
                if t == 0:
                    dve.wait_ge(s_xc, n_xc.after(it, "RES_ROW"))
                    if it.batch("A") >= 1:
                        dve.wait_ge(s_skip, n_skip.after(it.back(1), "SKIP"))
                V.scalar_tensor_tensor(x2[:, t, :], bank0[:, 0:H], post_f[:], xc[:, t, :],
                                       ALU.mult, ALU.add).then_inc(s_b0_done, 1)

            def gate_proj(it, par, t):
                dve.wait_ge(s_b1_full, n_b1.after(it, "GATE", t))
                if t == 0 and it.batch("A") >= 1:
                    dve.wait_ge(s_gtanh, n_gtanh.after(it.back(1), "GATE_TANH"))
                V.scalar_tensor_tensor(gpre[:, t, :], bank1[:, 0:H], post[:, WG:WG + 1], gate_b_row[:],
                                       ALU.mult, ALU.add).then_inc(s_b1_done, 1)

            def score_sum(it, par, _):
                dve.wait_ge(s_prod, n_prod.after(it, "SCORE_PROD"))
                for i, dst_ in enumerate((s8[par], nd)):
                    V.reduce_sum(dst_[:].rearrange("p t h -> p (t h)"),
                                 prod[:, i].rearrange("p t (h e) -> p (t h) e", e=D1), AX_X).then_inc(s_sd, 1)
                dve.wait_ge(s_sd, n_sd.after(it, "SCORE_SUM", 0, 2))
                V.tensor_copy(nd_parts[:, :, 0, :], nd[:]).then_inc(s_sd, 1)
                dve.wait_ge(s_sd, n_sd.after(it, "SCORE_SUM", 0, 3))
                V.tensor_tensor(nd_r[:], nd[:], nd_parts[:, :, 0, :], ALU.subtract).then_inc(s_sd, 1)
                dve.wait_ge(s_sd, n_sd.after(it, "SCORE_SUM", 0, 4))
                V.tensor_copy(nd_parts[:, :, 1, :], nd_r[:]).then_inc(s_nd, 1)
                dve.wait_ge(s_nd, n_nd.after(it, "SCORE_SUM"))
                V.tensor_tensor(nd_parts[:, :, 2, :], nd_r[:], nd_parts[:, :, 1, :], ALU.subtract).then_inc(s_sd, 1)

            def dst_t(it, par, _):
                dve.wait_ge(s_b1_full, n_b1.after(it, "DST_T"))
                V.tensor_copy(ndT[par][0:3 * H1, :], bank1[:].bitcast(BF16)[0:3 * H1, 0:T]).then_inc(s_b1_done, 1)

            def leaky1(it, par, u):
                c, t = divmod(u, 2)
                if t == 0:
                    dve.wait_ge(s_d5, n_db.after(it, "DST", c))
                if n_e1.some_before(it, "EXP1", u, 1):
                    dve.wait_ge(s_e1, n_e1.before(it, "EXP1", u, 1))
                for hh in range(2):
                    h = 2 * c + hh
                    V.scalar_tensor_tensor(yw[:, u % 2, hh, :], dst_ps[c % 2][:, hh * T:(hh + 1) * T],
                                           s8[par][:, t, h:h + 1], dst5[:, c % 2, hh, :],
                                           ALU.add, ALU.min).then_inc(s_lk, 1)
                for hh in range(2):
                    written = ready(dve, n_lk.after(it, "LEAKY1", u, hh + 1))
                    dve.wait_ge(s_pool_const, 8)
                    dve.wait_ge(s_lk, written)
                    last = V.tensor_tensor_reduce(y1[:, u % 2, hh, :], yw[:, u % 2, hh, :], mask[par][:, t, :],
                                                  1.0, 3.0e38, ALU.add, ALU.min, min1[:, u, hh:hh + 1])
                last.then_inc(s_y1, 1)

            def recip1(it, par, _):
                dve.wait_ge(s_e1, n_e1.after(it.back(1), "EXP1", 11))
                V.reciprocal(rec1[:].rearrange("p t h -> p (t h)"),
                             sum1[:].rearrange("p t h -> p (t h)")).then_inc(s_rec1, 1)

            def out_t(it, par, t):
                dve.wait_ge(s_b1_full, n_b1.after(it, "OUT_T", t))
                if t == 0:
                    dve.wait_ge(s_rec1, n_rec1.after(it, "RECIP1"))
                V.tensor_tensor(o1[:, t, :].rearrange("p (h e) -> p h e", e=D1),
                                bank1[:, 0:H].rearrange("p (h e) -> p h e", e=D1),
                                rec1[:, t, :].unsqueeze(2).broadcast_to([P, H1, D1]), ALU.mult).then_inc(s_b1_done, 1)

            def finish(it, par, _):
                dve.wait_ge(s_oe, n_oe.after(it, "ELU_EXP"))
                if it.batch("C") >= 1:
                    dve.wait_ge(s_out, n_out.after(it.back(1), "STORE"))
                V.scalar_tensor_tensor(ya[:], o1[:], 0.0, o1m[:], ALU.max, ALU.add).then_inc(s_fin, 1)
                dve.wait_ge(s_fin, n_fin.after(it, "FINISH", 0, 1))
                V.scalar_tensor_tensor(yb[:], ya[:], -1.0, hskip[par][:], ALU.add, ALU.subtract).then_inc(s_fin, 1)
                dve.wait_ge(s_fin, n_fin.after(it, "FINISH", 0, 2))
                V.scalar_tensor_tensor(ya[:], gate[par][:], 1.0, yb[:], ALU.add, ALU.mult).then_inc(s_fin, 1)
                dve.wait_ge(s_fin, n_fin.after(it, "FINISH", 0, 3))
                V.scalar_tensor_tensor(yb[:], ya[:], 0.5, xskip[par][:], ALU.mult, ALU.add).then_inc(s_fin, 1)

            walk(dve, {"STATS0": stats(xb, 0, "STATS0"), "NORM0": norm(xb, 0, "NORM0", "RSTD0"), "LN_T0": ln_t0,
                       "QK": qk, "QK0": qk0, "NORMP0": normp0, "PV0": pv0, "OUT0": out0,
                       "STATS1": stats(x2, 1, "STATS1"), "NORM1": norm(x2, 1, "NORM1", "RSTD1"), "LN_T1": ln_t1,
                       "GATE": gate_proj, "SCORE_SUM": score_sum, "DST_T": dst_t, "LEAKY1": leaky1,
                       "RECIP1": recip1, "OUT_T": out_t, "FINISH": finish})

        @block.gpsimd
        def _(pool):
            G = nc.gpsimd
            G.memset(ident[:], 0.0).then_inc(s_pool_const, 1)
            G.memset(pick[:], 0.0).then_inc(s_pool_const, 1)
            G.memset(half[:], -0.5).then_inc(s_pool_const, 1)
            pool.wait_ge(s_pool_const, 3)
            G.affine_select(out=ident[:], in_=ident[:], compare_op=ALU.not_equal, fill=1.0, base=0,
                            pattern=[[-1, P]], channel_multiplier=1).then_inc(s_pool_const, 1)
            for i in range(3):
                G.affine_select(out=pick[:], in_=pick[:], compare_op=ALU.not_equal, fill=1.0, base=-H1 * i,
                                pattern=[[-1, H1], [0, P]], channel_multiplier=1).then_inc(s_pool_const, 1)
                pool.wait_ge(s_pool_const, 5 + i)
            for i in range(2):
                G.memset(kz[i][:], 0.0)
                G.memset(ndT[i][:], 0.0)
            G.tensor_copy(ident_b[:], ident[:]).then_inc(s_pool_const, 1)
            for w in range(6):
                pool.wait_ge(s_wmax, w + 1)
                G.partition_all_reduce(wmax_all[:, w:w + 1], wmax[:, w:w + 1], P, RMAX).then_inc(s_wmax_all, 1)

            def mask_(it, par, _):
                here = ready(pool, loaded(it, "P"))
                read = ready(pool, n_y1.after(it, "LEAKY1", 11)) if it.batch("P") >= 2 else None
                pool.wait_ge(s_pool_const, 8)
                pool.wait_ge(s_adj[par], here)
                if it.batch("P") >= 2:
                    pool.wait_ge(s_y1, read)
                G.tensor_scalar(mask[par][:], adj_raw[par][:], -1.0, -BIG, ALU.add, ALU.mult).then_inc(s_mask, 1)

            def rstd_(k, step, sstep):
                def part(it, par, _):
                    here = ready(pool, n_mv.after(it, sstep))
                    pool.wait_ge(s_pool_const, 8)
                    pool.wait_ge(s_mv, here)
                    G.tensor_scalar(veps[:, k, :], mv[k][:, :, 1], EPS, XS ** -2, ALU.add, ALU.mult).then_inc(s_veps, 1)
                    pool.wait_ge(s_veps, n_veps.after(it, step))
                    G.tensor_tensor(rstd[k][:], veps[:, k, :], half[:], ALU.pow).then_inc(s_rstd, 1)
                return part

            def normp0(it, par, u):
                here = ready(pool, n_np0.after(it, "NORMP0", u))
                pool.wait_ge(s_pool_const, 8)
                pool.wait_ge(s_rec0, here)
                for hh in range(2):
                    last = G.tensor_scalar(p0[:, u % 3, hh, :], p0[:, u % 3, hh, :], rec0[:, u, hh:hh + 1], 1.0,
                                           ALU.mult, ALU.mult)
                last.then_inc(s_p0, 1)

            def res_row(it, par, _):
                pool.wait_ge(s_x[par], loaded(it, "A"))
                if it.batch("A") == 0:
                    pool.wait_ge(s_rowdone, 1)
                else:
                    pool.wait_ge(s_b0_done, n_b0.after(it.back(1), "OUT0", 1))
                G.tensor_tensor(xc[:], xb[par][:], out0_row[:].unsqueeze(1).broadcast_to([P, NT, H]),
                                ALU.add).then_inc(s_xc, 1)

            def score_prod(it, par, _):
                pool.wait_ge(s_th, n_th.after(it, "HEADS", 1))
                if it.batch("A") >= 1:
                    pool.wait_ge(s_sd, n_sd.after(it.back(1), "SCORE_SUM"))
                else:
                    pool.wait_ge(s_setup, 3)
                for i, row in enumerate((src_row, dst_row)):
                    last = G.tensor_tensor(prod[:, i], th[:], row[:].unsqueeze(1).broadcast_to([P, NT, H]), ALU.mult)
                last.then_inc(s_prod, 1)

            def skip(it, par, _):
                here = ready(pool, n_norm.after(it, "NORM1"))
                used = ready(pool, n_fin.after(it, "FINISH")) if it.batch("A") >= 2 else None
                pool.wait_ge(s_pool_const, 8)
                pool.wait_ge(s_norm, here)
                if it.batch("A") >= 2:
                    pool.wait_ge(s_fin, used)
                G.tensor_scalar(hskip[par][:], xn[1][:], 0.0, 1.0 / XS, ALU.max, ALU.mult).then_inc(s_skip, 1)
                pool.wait_ge(s_skip, n_skip.after(it, "SKIP", 0, 1))
                G.tensor_tensor(xskip[par][:], hskip[par][:], x2[:], ALU.add).then_inc(s_skip, 1)

            def elu_min(it, par, _):
                pool.wait_ge(s_b1_done, n_b1.after(it, "OUT_T", 1))
                G.tensor_tensor(o1[:].rearrange("p t (h e) -> p (t h) e", e=D1),
                                o1[:].rearrange("p t (h e) -> p (t h) e", e=D1),
                                gat_b_row[:].unsqueeze(1).broadcast_to([P, NT * H1, D1]), ALU.add).then_inc(s_om, 1)
                written = ready(pool, n_om.after(it, "ELU_MIN", 0, 1))
                pool.wait_ge(s_pool_const, 8)
                pool.wait_ge(s_om, written)
                G.tensor_scalar(o1m[:], o1[:], 0.0, 0.0, ALU.min, ALU.add).then_inc(s_om, 1)

            walk(pool, {"MASK": mask_, "RSTD0": rstd_(0, "RSTD0", "STATS0"), "RSTD1": rstd_(1, "RSTD1", "STATS1"),
                        "NORMP0": normp0, "RES_ROW": res_row, "SCORE_PROD": score_prod, "SKIP": skip,
                        "ELU_MIN": elu_min})


SETUP_SCALES = 3 + 6 * 6 + 4

_INS = ["x", "adj", "w_all", "bq", "bk", "bv", "bf", "gat_b", "w_src", "w_dst", "gate_b"]


def kernel(x, adj, L0_gnn_Wq, L0_gnn_bq, L0_gnn_Wk, L0_gnn_bk, L0_gnn_Wv, L0_gnn_bv, L0_gnn_Wf, L0_gnn_bf,
           L1_gnn_W, L1_gnn_b, L1_gnn_w_src, L1_gnn_w_dst, L1_gnn_H_w, L1_gnn_H_b):
    import concourse.bacc as bacc
    from concourse.bass_utils import run_bass_kernel_spmd

    heads_w = np.asarray(L1_gnn_W).transpose(1, 0, 2).reshape(H, H)


    def columns(a):
        return np.asarray(a).reshape(NC, P).T

    given = {
        "x": x, "adj": adj,
        "w_all": np.stack([np.asarray(L0_gnn_Wq), np.asarray(L0_gnn_Wk), np.asarray(L0_gnn_Wv),
                           np.asarray(L0_gnn_Wf), heads_w, np.asarray(L1_gnn_H_w).T]),
        "bq": columns(L0_gnn_bq), "bk": columns(L0_gnn_bk), "bv": columns(L0_gnn_bv), "bf": L0_gnn_bf, "gat_b": L1_gnn_b,
        "w_src": np.asarray(L1_gnn_w_src).reshape(H), "w_dst": np.asarray(L1_gnn_w_dst).reshape(H),
        "gate_b": L1_gnn_H_b,
    }
    nc = bacc.Bacc("TRN2", target_bir_lowering=False, num_devices=1)
    arrays, args = {}, []
    for name in _INS:
        a = np.ascontiguousarray(given[name])
        arrays[f"in_{name}_dram"] = a
        args.append(nc.dram_tensor(f"in_{name}_dram", a.shape, mybir.dt.from_np(a.dtype), kind="ExternalInput").ap())
    out = nc.dram_tensor("out_dram", np.asarray(x).shape, F32, kind="ExternalOutput").ap()
    build(nc, *args, out)
    r = run_bass_kernel_spmd(nc, [arrays], core_ids=[0])
    return r.results[0]["out_dram"]
```

```python
from contextlib import ExitStack

import numpy as np

import concourse.bass as bass
from concourse import mybir

F32, F16, BF16, U8 = mybir.dt.float32, mybir.dt.float16, mybir.dt.bfloat16, mybir.dt.uint8
ALU = mybir.AluOpType
ACT = mybir.ActivationFunctionType
AX_X = mybir.AxisListType.X
RMAX = bass.bass_isa.ReduceOp.max

P = 128
T = 256
H = 384
NT = T // P
NC = H // P
H0, D0 = 6, 64
H1, D1 = 12, 32
BIG = 9.0e15
ALPHA = 0.2
EPS = 1e-5
XS = 1024.0
WS = 16384.0
VS = 2.0 ** -17
WQ, WK, WV, WF, WH, WG = range(6)
YB = 3
TERMS = ((0, 0), (0, 1), (1, 0))


FILL = {
    0: [("P", "STATS0", 0), ("P", "RSTD0", 0), ("B", "GATE", 0), ("B", "SCORE_PROD", 0)],
    1: [("P", "NORM0", 0), ("B", "GATE", 1)],
    2: [("P", "LN_T0", 0), ("C", "PV1", 2), ("B", "SCORE_SUM", 0), ("C", "RECIP1", 0)],
    3: [("P", "LN_T0", 1), ("B", "DST_T", 0), ("B", "GATE_TANH", 0), ("B", "MASK1", 0)],
    4: [("C", "OUT_T", 0), ("A", "PV0", 0), ("B", "SKIP_H", 0), ("P", "LOAD_ADJ", 0)],
    5: [("C", "OUT_T", 1), ("P", "Q", 0)],
    6: [("P", "K", 0), ("A", "PV0", 1), ("C", "ELU_BIAS", 0)],
    7: [("P", "Q", 1), ("C", "ELU_EXP", 0), ("A", "RES_ROW", 0)],
    8: [("P", "K", 1), ("A", "PV0", 2), ("C", "FINISH", 0), ("P", "MASK0", 0)],
    9: [("P", "Q", 2), ("C", "FINISH", 1), ("B", "GATES", 0)],
    10: [("A", "OUT0", 0), ("C", "OUT_SUM", 0), ("C", "STORE", 0)],
    11: [("A", "OUT0", 1), ("B", "SKIP", 0)],
    12: [("P", "K", 2), ("B", "PV1", 0), ("A", "STATS1", 0), ("A", "RSTD1", 0), ("L", "LOAD_X", 0)],
    13: [("P", "V", 0), ("A", "NORM1", 0)],
    14: [("A", "LN_T1", 0), ("A", "LN_T1", 1)],
    15: [("P", "V", 1)],
    16: [("A", "HEADS", 0), ("B", "PV1", 1)],
    17: [("A", "HEADS", 1)],
}
JOBS = {"LN_T0": 1, "Q": 1, "K": 1, "V": 1, "PV0": 1, "OUT0": 1, "LN_T1": 1, "HEADS": 1, "GATE": 1,
        "DST_T": 1, "PV1": 1, "OUT_T": 1}
LATER = {"L": "P", "P": "A", "A": "B", "B": "C", "C": "D"}


def order_of_steps():
    units = [("A", u) for u in range(6)] + [("B", u) for u in range(12)]
    n = len(units)

    def unit(slot):
        ph, u = units[slot % n]
        return (ph if slot >= 0 else LATER[ph]), u, ph == "A"

    made, taken = [], []
    for slot in range(n):
        steps = []
        ph, u, block0 = unit(slot - 3)
        steps.append((ph, "PT0" if block0 else "PT1", u))
        if slot + 1 < n and units[slot + 1][0] == "B" and units[slot + 1][1] % 2 == 0:
            steps.append(("B", "DST", units[slot + 1][1] // 2))
        ph, u, block0 = unit(slot - 2)
        if block0:
            steps.append((ph, "NORMP0", u))
        ph, u, block0 = unit(slot - 1)
        steps.append((ph, "EXP0" if block0 else "EXP1", u))
        ph, u, block0 = unit(slot)
        steps.append((ph, "QK0" if block0 else "LEAKY1", u))
        made += steps + FILL[slot]
        before = FILL[(slot - 1) % n]
        taken += steps + [(LATER[ph] if slot == 0 else ph, step, idx) for ph, step, idx in before if step in JOBS]
        taken += [s for s in FILL[slot] if s[1] not in JOBS]
    return made, taken


ORDER, ORDER_TAKEN = order_of_steps()
LAG = {"L": -2, "P": -1, "A": 0, "B": 1, "C": 2, "D": 3}


class Batch:

    def __init__(self, ref, reg=None):
        self.ref, self.reg = ref, reg

    def back(self, k):
        return Batch(self.ref - k, self.reg)

    def value(self):
        return self.ref if self.reg is None else self.reg * 2 + self.ref


class Count:

    def __init__(self, n_batch, per_step, unit=1):
        self.per_step, self.unit, self.n = per_step, unit, n_batch
        self.starts = {-2: 0}
        for it in range(-2, n_batch + 3):
            self.starts[it + 1] = self.starts[it] + sum(per_step[s] for ph, s, _ in ORDER if self._on(ph, it, s))
        self.per = self.starts[3] - self.starts[2]

    def _on(self, phase, it, step):
        return step in self.per_step and 0 <= it - LAG[phase] < self.n

    def _ahead(self, batch, step, idx):
        assert 0 <= batch.ref < self.n, (step, batch.ref)
        it = batch.ref + next(LAG[ph] for ph, s, i in ORDER if (s, i) == (step, idx))
        n = self.starts[it]
        for ph, s, i in ORDER:
            if (s, i) == (step, idx):
                return n
            if self._on(ph, it, s):
                n += self.per_step[s]

    def _value(self, batch, n):
        v = n * self.unit
        return v if batch.reg is None else batch.reg * (2 * self.per * self.unit) + v

    def before(self, batch, step, idx=0, less=0):
        return self._value(batch, self._ahead(batch, step, idx) - less)

    def some_before(self, batch, step, idx=0, less=0):
        return self._ahead(batch, step, idx) - less > 0

    def after(self, batch, step, idx=0, k=None):
        return self._value(batch, self._ahead(batch, step, idx) + (self.per_step[step] if k is None else k))


class Jobs(Count):
    BANKS = 3

    def __init__(self, n_batch):
        super().__init__(n_batch, JOBS)
        assert 2 * self.per % self.BANKS == 0

    def bank(self, batch, step, idx):
        return self._ahead(batch, step, idx) % self.BANKS

    def used(self, batch, step, idx):
        return self._ahead(batch, step, idx) >= self.BANKS

    def before(self, batch, step, idx=0):
        v = self._ahead(batch, step, idx) // self.BANKS
        return v if batch.reg is None else batch.reg * (2 * self.per // self.BANKS) + v

    def after(self, batch, step, idx=0):
        return self.before(batch, step, idx) + 1


def build(nc, x, adj, w_all, bq, bk, bv, bf, gat_b, w_src, w_dst, gate_b, out):
    NB = x.shape[0]
    LOOP = (NB - 4) // 2
    assert NB % 2 == 0 and LOOP >= 1

    x_v = x.rearrange("b (t p) h -> b p t h", p=P)
    out_v = out.rearrange("b (t p) h -> b p t h", p=P)
    adj_v = adj.rearrange("b (t p) m -> b p t m", p=P)
    w_v = w_all.rearrange("w (c p) n -> w p c n", p=P)

    with ExitStack() as ctx:
        def sb(name, shape, dt=F32):
            return ctx.enter_context(nc.sbuf_tensor(name, shape, dt))

        def sem(name):
            return ctx.enter_context(nc.semaphore(name))

        def banks(name, n):
            return [ctx.enter_context(nc.psum_tensor(f"{name}{i}", [P, 512], F32)) for i in range(n)]

        job_ps = banks("job", Jobs.BANKS)
        unit_ps = banks("unit", 3)
        pt_ps = banks("pt", 2)

        w16 = sb("w16", [P, 6, 2, NC, H], F16)
        wmax = sb("wmax", [P, 6])
        wmax_all = sb("wmax_all", [P, 6])
        wscale = sb("wscale", [P, 6])
        post = sb("post", [P, 6])
        post_q = sb("post_q", [P, 1])
        post_f = sb("post_f", [P, 1])
        bq_c = sb("bq_c", [P, NC])
        bk_c = sb("bk_c", [P, NC])
        bv_c = sb("bv_c", [P, NC])
        bv_w = sb("bv_w", [P, NC, P])
        out0_row = sb("out0_row", [P, H])
        gat_b_row = sb("gat_b_row", [P, D1])
        gate_b_row = sb("gate_b_row", [P, H])
        src_row = sb("src_row", [P, H])
        dst_row = sb("dst_row", [P, H])
        ident = sb("ident", [P, P])
        ident_b = sb("ident_b", [P, P], BF16)
        pick = sb("pick", [P, H1, P], BF16)
        half = sb("half", [P, NT])

        xb = [sb(f"xb{i}", [P, NT, H]) for i in range(2)]
        adj_raw = [sb(f"adj_raw{i}", [P, NT, T], U8) for i in range(2)]
        mask0 = sb("mask0", [P, NT, T])
        mask1 = sb("mask1", [P, NT, T])
        bn = sb("bn", [P, NT, 6])
        mv = [sb(f"mv{i}", [P, NT, 2]) for i in range(2)]
        veps = sb("veps", [P, 2, NT])
        rstd = [sb(f"rstd{i}", [P, NT]) for i in range(2)]
        xn = [sb(f"xn{i}", [P, NT, H]) for i in range(2)]
        h16 = [sb(f"h16_{i}", [P, 2, NC, T], F16) for i in range(2)]
        qT = [sb(f"qT{i}", [P, 3, T]) for i in range(2)]
        kz = [sb(f"kz{i}", [P, H0, T]) for i in range(2)]
        vv = [sb(f"vv{i}", [P, NT, H]) for i in range(2)]
        y0 = sb("y0", [P, YB, 2, T])
        p0 = sb("p0", [P, 3, 2, T])
        min0 = sb("min0", [P, 6, 2])
        sum0 = sb("sum0", [P, 6, 2])
        rec0 = sb("rec0", [P, 6, 2])
        pT0 = sb("pT0", [P, 2, 2, NT, T])
        c16 = sb("c16", [P, 2, 3, T], F16)
        xc = sb("xc", [P, NT, H])
        x2 = [sb(f"x2_{i}", [P, NT, H]) for i in range(2)]
        th = sb("th", [P, NT, H])
        prod = sb("prod", [P, 2, NT, H])
        hv = [sb(f"hv{i}", [P, NT, H]) for i in range(2)]
        s8 = [sb(f"s8_{i}", [P, NT, H1]) for i in range(2)]
        nd = sb("nd", [P, NT, H1])
        nd_r = sb("nd_r", [P, NT, H1])
        nd_parts = sb("nd_parts", [P, NT, 3, H1], BF16)
        ndT = [sb(f"ndT{i}", [P, T], BF16) for i in range(2)]
        gpre = sb("gpre", [P, NT, H])
        gtanh = sb("gtanh", [P, NT, H])
        gate = [sb(f"gate{i}", [P, NT, H]) for i in range(2)]
        ungate = sb("ungate", [P, NT, H])
        hskip = sb("hskip", [P, NT, H])
        xskip = [sb(f"xskip{i}", [P, NT, H]) for i in range(2)]
        dst5 = sb("dst5", [P, 2, 2, T])
        yw = sb("yw", [P, 2, 2, T])
        y1 = sb("y1", [P, YB, 2, T])
        p1 = sb("p1", [P, 3, 2, T])
        min1 = sb("min1", [P, 12, 2])
        sum1 = sb("sum1", [P, NT, H1])
        rec1 = sb("rec1", [P, NT, H1])
        pT1 = sb("pT1", [P, 2, 4, NT, T])
        setup_room = pT1[:].rearrange("p a q k t -> p (a q k t)")
        wstage = setup_room[:, 0:2 * NC * H].rearrange("p (w c n) -> p w c n", w=2, c=NC)
        wabs = setup_room[:, 2 * NC * H:3 * NC * H].rearrange("p (c n) -> p c n", c=NC)
        oT = sb("oT", [P, 3, T])
        o1 = sb("o1", [P, NT, H])
        o1m = sb("o1m", [P, NT, H])
        y = sb("y", [P, NT, H])

        s_w = [sem(f"s_weight{i}") for i in range(6)]
        s_small = sem("s_small_inputs")
        s_wmax = sem("s_wmax")
        s_wmax_all = sem("s_wmax_all")
        s_w16 = sem("s_w16")
        s_setup = sem("s_setup_dve")
        s_setup_act = sem("s_setup_act")
        s_pool_const = sem("s_pool_const")
        s_bvw = sem("s_bvw")
        s_row = sem("s_row")
        s_rowdone = sem("s_rowdone")

        s_x = [sem(f"s_x_loaded{i}") for i in range(2)]
        s_adj = [sem(f"s_adj_loaded{i}") for i in range(2)]
        n_job = Jobs(NB)
        s_full = [sem(f"s_job_made{i}") for i in range(Jobs.BANKS)]
        s_done = [sem(f"s_job_taken{i}") for i in range(Jobs.BANKS)]
        s_mask0, n_mask0 = sem("s_mask0"), Count(NB, {"MASK0": 1})
        s_mask1, n_mask1 = sem("s_mask1"), Count(NB, {"MASK1": 1})
        s_bn, n_bn = sem("s_bn_stats"), Count(NB, {"STATS0": 1, "STATS1": 1})
        s_mv, n_mv = sem("s_mean_var"), Count(NB, {"STATS0": 1, "STATS1": 1})
        s_veps, n_veps = sem("s_veps"), Count(NB, {"RSTD0": 1, "RSTD1": 1})
        s_rstd, n_rstd = sem("s_rstd"), Count(NB, {"RSTD0": 1, "RSTD1": 1})
        s_norm, n_norm = sem("s_normalised"), Count(NB, {"NORM0": 1, "NORM1": 1})
        s_q, n_q = sem("s_q_in_sbuf"), Count(NB, {"Q": 1})
        s_hi0, n_hi0 = sem("s_high_part0"), Count(NB, {"LN_T0": 1, "PV0": 1})
        s_hi1, n_hi1 = sem("s_high_part1"), Count(NB, {"LN_T1": 1})
        s_s0, n_s0 = sem("s_scores0"), Count(NB, {"QK0": 1})
        s_y0 = sem("s_masked0")
        s_e0, n_e0 = sem("s_exp0"), Count(NB, {"EXP0": 1})
        s_rec0, n_np0 = sem("s_reciprocal0"), Count(NB, {"NORMP0": 1})
        s_p0 = sem("s_probs0")
        s_t, n_t = sem("s_probs_transposed"), Count(NB, {"PT0": 1, "PT1": 1})
        s_pT = sem("s_pT_in_sbuf")
        s_xc, n_xc = sem("s_residual_row"), Count(NB, {"RES_ROW": 1})
        s_th, n_th = sem("s_tanh_heads"), Count(NB, {"HEADS": 1})
        s_prod, n_prod = sem("s_score_products"), Count(NB, {"SCORE_PROD": 1})
        s_sd, n_sd = sem("s_score_parts"), Count(NB, {"SCORE_SUM": 5})
        s_nd, n_nd = sem("s_dst_middle_part"), Count(NB, {"SCORE_SUM": 1})
        s_gtanh, n_gtanh = sem("s_gate_tanh"), Count(NB, {"GATE_TANH": 1})
        s_hskip, n_hskip = sem("s_skip_h"), Count(NB, {"SKIP_H": 1})
        s_gate, n_gate = sem("s_gates"), Count(NB, {"GATES": 1})
        s_ungate, n_ungate = sem("s_ungated_h"), Count(NB, {"SKIP": 1})
        s_skip, n_skip = sem("s_skip"), Count(NB, {"SKIP": 1})
        s_db, n_db = sem("s_dst_rows"), Count(NB, {"DST": 1})
        s_d5 = sem("s_dst_rows_scaled")
        s_lk, n_lk = sem("s_leaky"), Count(NB, {"LEAKY1": 2})
        s_y1, n_y1 = sem("s_masked1"), Count(NB, {"LEAKY1": 1})
        s_e1, n_e1 = sem("s_exp1"), Count(NB, {"EXP1": 1})
        s_rec1, n_rec1 = sem("s_reciprocal1"), Count(NB, {"RECIP1": 1})
        s_ob, n_ob = sem("s_elu_bias"), Count(NB, {"ELU_BIAS": 1})
        s_om, n_om = sem("s_elu_negative"), Count(NB, {"ELU_EXP": 1})
        s_oe, n_oe = sem("s_elu_exp"), Count(NB, {"ELU_EXP": 1})
        s_fin, n_fin = sem("s_finish"), Count(NB, {"FINISH": 1})
        s_sum, n_sum = sem("s_output_rows"), Count(NB, {"OUT_SUM": 1})
        s_out, n_out = sem("s_stored"), Count(NB, {"STORE": 1}, 16)

        def ready(eng, value):
            if isinstance(value, int):
                return value
            if eng.engine not in count_regs:
                count_regs[eng.engine] = [eng.alloc_register(f"count{i}_{eng.engine.name}") for i in range(3)]
            regs = count_regs[eng.engine]
            regs.append(regs.pop(0))
            eng.reg_mov(regs[-1], value)
            return regs[-1]

        count_regs = {}

        def loaded(b):
            v = 16 * (b.ref // 2 + 1)
            return v if b.reg is None else b.reg * 16 + v

        def job(b, step, idx=0):
            i = n_job.bank(b, step, idx)
            return job_ps[i], s_full[i], s_done[i], n_job.after(b, step, idx)

        def walk(eng, parts, order=ORDER_TAKEN):
            def iteration(it, reg=None):
                for phase, step, idx in order:
                    b = Batch(it - LAG[phase], reg)
                    if step in parts and 0 <= b.ref < NB:
                        parts[step](b, b.ref % 2, idx)
            for n in range(-2, 2):
                iteration(n)
            with eng.Fori(0, LOOP) as j:
                iteration(2, j)
                iteration(3, j)
            for n in range(NB - 2, NB + 3):
                iteration(n)

        block = ctx.enter_context(nc.Block())

        @block.sync
        def _(sp):
            small = [
                (bq_c[:], bq), (bk_c[:], bk),
                (bv_c[:], bv),
                (out0_row[:], bf.partition_broadcast(P)), (gat_b_row[:], gat_b.partition_broadcast(P)),
                (gate_b_row[:], gate_b.partition_broadcast(P)), (src_row[:], w_src.partition_broadcast(P)),
                (dst_row[:], w_dst.partition_broadcast(P)),
            ]
            for w in range(2):
                sp.dma_start(wstage[:, w], w_v[w]).then_inc(s_w[w], 16)
            for dst, src in small:
                sp.dma_start(dst, src).then_inc(s_small, 16)
            for w in range(2, 6):
                sp.wait_ge(s_w16, w - 1)
                sp.dma_start(wstage[:, w % 2], w_v[w]).then_inc(s_w[w], 16)

            def of_batch(view, b, rows):
                return view[b.value()] if b.reg is None else view[bass.ds(b.value(), 1)].rearrange(rows)

            def load_x(b, par, _):
                x_b = of_batch(x_v, b, "a p t h -> (a p) t h")
                if b.ref >= 2:
                    sp.wait_ge(s_norm, n_norm.after(b.back(2), "NORM0"))
                    sp.wait_ge(s_xc, n_xc.after(b.back(2), "RES_ROW"))
                sp.dma_start(xb[par][:], x_b).then_inc(s_x[par], 16)

            def load_adj(b, par, _):
                adj_b = of_batch(adj_v, b, "a p t m -> (a p) t m")
                if b.ref >= 2:
                    used = ready(sp, n_mask1.after(b.back(2), "MASK1"))
                    sp.wait_ge(s_pool_const, 8)
                    sp.wait_ge(s_mask1, used)
                sp.dma_start(adj_raw[par][:], adj_b).then_inc(s_adj[par], 16)

            def store(b, par, _):
                out_b = of_batch(out_v, b, "a p t h -> (a p) t h")
                sp.wait_ge(s_sum, n_sum.after(b, "OUT_SUM"))
                sp.dma_start(out_b, y[:]).then_inc(s_out, 16)

            walk(sp, {"LOAD_X": load_x, "LOAD_ADJ": load_adj, "STORE": store})
            sp.wait_ge(s_out, 16 * NB)

        @block.tensor
        def _(pe):
            mm = nc.tensor.matmul

            pe.wait_ge(s_w[WF], 16)
            pe.wait_ge(s_bvw, 1)
            for c in range(NC):
                last = mm(job_ps[0][:, 0:H], bv_w[:, c, :], wstage[:, WF % 2, c, :], start=c == 0, stop=c == NC - 1)
            last.then_inc(s_row, 1)
            pe.wait_ge(s_rowdone, 1)
            pe.wait_ge(s_pool_const, 8)
            pe.wait_ge(s_w16, 6)

            def bank_free(b, step, idx, needs=()):
                bank, made, taken, _ = job(b, step, idx)
                wait_taken(b, needs, n_job.bank(b, step, idx))
                if n_job.used(b, step, idx):
                    pe.wait_ge(taken, n_job.before(b, step, idx))
                return bank, made

            def wait_taken(b, needs, but=None):
                last = {n_job.bank(b, step, idx): (step, idx) for step, idx in needs}
                for bank, (step, idx) in last.items():
                    if bank != but:
                        pe.wait_ge(s_done[bank], n_job.after(b, step, idx))

            def transpose_norm(bank, src, k):
                for i, c in enumerate((0, 1) if k == 0 else (2,)):
                    for t in range(NT):
                        last = nc.tensor.transpose(bank[:, i * T + t * P:i * T + (t + 1) * P],
                                                   src[:, t, c * P:(c + 1) * P], ident[:])
                return last

            def to_rows(bank, rows, t, w):
                n = 0
                for c in range(NC):
                    for i, j in TERMS:
                        last = mm(bank[:, 0:H], rows[:, i, c, t * P:(t + 1) * P], w16[:, w, j, c, :],
                                  start=n == 0, stop=n == 3 * NC - 1)
                        n += 1
                return last

            def to_columns(step, w):
                def part(b, par, p):
                    bank, made = bank_free(b, step, p, (("LN_T0", 0), ("LN_T0", 1)) if (step, p) == ("Q", 0) else ())
                    n = 0
                    for c in range(NC):
                        for i, j in TERMS:
                            last = mm(bank[:, 0:T], w16[:, w, i, c, p * P:(p + 1) * P], h16[0][:, j, c, :],
                                      start=n == 0, stop=n == 3 * NC - 1)
                            n += 1
                    last.then_inc(made, 1)
                return part

            def ln_t0(b, par, k):
                if k == 0:
                    pe.wait_ge(s_norm, n_norm.after(b, "NORM0"))
                bank, made = bank_free(b, "LN_T0", k)
                transpose_norm(bank, xn[0], k).then_inc(made, 1)

            def v(b, par, t):
                bank, made = bank_free(b, "V", t)
                to_rows(bank, h16[0], t, WV).then_inc(made, 1)

            def qk0(b, par, u):
                p, qt = divmod(u, 2)
                if qt == 0:
                    wait_taken(b, (("Q", p), ("K", p)))
                if u >= 3:
                    pe.wait_ge(s_y0, n_s0.after(b, "QK0", u - 3))
                elif b.ref >= 2:
                    pe.wait_ge(s_y1, n_y1.after(b.back(2), "LEAKY1", 2 * u + 7))
                elif b.ref == 1:
                    pe.wait_ge(s_y0, n_s0.after(b.back(1), "QK0", u + 3))
                mm(unit_ps[u % 3][:], qT[par][:, p, qt * P:(qt + 1) * P], kz[par][:, 2 * p:2 * p + 2, :],
                   start=True, stop=True).then_inc(s_s0, 1)

            def dst(b, par, c):
                if c == 0:
                    wait_taken(b, (("DST_T", 0),))
                if c >= 3:
                    pe.wait_ge(s_y1, n_y1.after(b, "LEAKY1", 2 * c - 5))
                elif b.ref + 1 < NB:
                    pe.wait_ge(s_y0, n_s0.after(b.back(-1), "QK0", c + 3))
                else:
                    pe.wait_ge(s_y1, n_y1.after(b.back(1), "LEAKY1", 2 * c + 7))
                for hh in range(2):
                    last = mm(unit_ps[c % 3][:, hh * T:(hh + 1) * T], pick[:, 2 * c + hh, :], ndT[par][:],
                              start=True, stop=True)
                last.then_inc(s_db, 1)

            def transpose_probs(b, step, u, probs):
                if n_t.some_before(b, step, u, 1):
                    pe.wait_ge(s_pT, n_t.before(b, step, u, 1))
                for hh in range(2):
                    for kt in range(NT):
                        last = nc.tensor.transpose(pt_ps[u % 2][:, (2 * hh + kt) * P:(2 * hh + kt + 1) * P],
                                                   probs[:, u % 3, hh, kt * P:(kt + 1) * P], ident[:])
                last.then_inc(s_t, 1)

            def pt0(b, par, u):
                pe.wait_ge(s_p0, n_np0.after(b, "NORMP0", u))
                transpose_probs(b, "PT0", u, p0)

            def pt1(b, par, u):
                pe.wait_ge(s_e1, n_e1.after(b, "EXP1", u))
                transpose_probs(b, "PT1", u, p1)

            def pv0(b, par, p):
                pe.wait_ge(s_pT, n_t.after(b, "PT0", 2 * p + 1))
                bank, made = bank_free(b, "PV0", p, (("V", 0), ("V", 1)) if p == 0 else ())
                for kt in range(NT):
                    for hh in range(2):
                        h = 2 * p + hh
                        last = mm(bank[D0 * hh:D0 * (hh + 1), 0:T], vv[par][:, kt, h * D0:(h + 1) * D0],
                                  pT0[:, p % 2, hh, kt, :], start=kt == 0, stop=kt == NT - 1)
                last.then_inc(made, 1)

            def out0(b, par, t):
                bank, made = bank_free(b, "OUT0", t, [("PV0", p) for p in range(3)] if t == 0 else ())
                to_rows(bank, c16, t, WF).then_inc(made, 1)

            def ln_t1(b, par, k):
                if k == 0:
                    pe.wait_ge(s_norm, n_norm.after(b, "NORM1"))
                bank, made = bank_free(b, "LN_T1", k)
                transpose_norm(bank, xn[1], k).then_inc(made, 1)

            def heads(b, par, t):
                bank, made = bank_free(b, "HEADS", t, (("LN_T1", 0), ("LN_T1", 1)) if t == 0 else ())
                to_rows(bank, h16[1], t, WH).then_inc(made, 1)

            def gate_proj(b, par, t):
                bank, made = bank_free(b, "GATE", t)
                to_rows(bank, h16[1], t, WG).then_inc(made, 1)

            def dst_t(b, par, _):
                bank, made, taken, _ = job(b, "DST_T")
                parts, free = ready(pe, n_sd.after(b, "SCORE_SUM")), ready(pe, n_job.before(b, "DST_T"))
                pe.wait_ge(s_pool_const, 8)
                pe.wait_ge(s_sd, parts)
                pe.wait_ge(taken, free)
                view = bank[:].bitcast(BF16)
                for t in range(NT):
                    last = nc.tensor.transpose(view[0:3 * H1, t * P:(t + 1) * P],
                                               nd_parts[:, t].rearrange("p a h -> p (a h)"), ident_b[:])
                last.then_inc(made, 1)

            def pv1(b, par, g):
                pe.wait_ge(s_pT, n_t.after(b, "PT1", 4 * g + 3))
                bank, made = bank_free(b, "PV1", g)
                for kt in range(NT):
                    for q in range(4):
                        h = 4 * g + q
                        last = mm(bank[D1 * q:D1 * (q + 1), 0:T], hv[par][:, kt, h * D1:(h + 1) * D1],
                                  pT1[:, g % 2, q, kt, :], start=kt == 0, stop=kt == NT - 1,
                                  tile_position=(0, D1 * q))
                last.then_inc(made, 1)

            def out_t(b, par, t):
                bank, made = bank_free(b, "OUT_T", t, [("PV1", g) for g in range(3)] if t == 0 else ())
                for g in range(3):
                    last = nc.tensor.transpose(bank[:, g * P:(g + 1) * P], oT[:, g, t * P:(t + 1) * P], ident[:])
                last.then_inc(made, 1)

            walk(pe, {"LN_T0": ln_t0, "Q": to_columns("Q", WQ), "K": to_columns("K", WK), "V": v, "QK0": qk0,
                      "PT0": pt0, "PV0": pv0, "OUT0": out0, "LN_T1": ln_t1, "HEADS": heads, "GATE": gate_proj,
                      "DST_T": dst_t, "DST": dst, "PT1": pt1, "PV1": pv1, "OUT_T": out_t}, ORDER)

        @block.scalar
        def _(act):
            op = nc.scalar.activation

            act.wait_ge(s_wmax_all, 1)
            act.wait_ge(s_setup, SETUP_SCALES)

            def made(b, step, idx=0):
                bank, full, taken, value = job(b, step, idx)
                act.wait_ge(full, value)
                return bank, taken

            def high_part(bank, h, k):
                c = slice(0, 2) if k == 0 else slice(2, 3)
                n = (c.stop - c.start) * T
                return op(h[:, 0, c, :], bank[:, 0:n].rearrange("p (c t) -> p c t", t=T), ACT.Relu)

            def ln_t0(b, par, k):
                high_part(made(b, "LN_T0", k)[0], h16[0], k).then_inc(s_hi0, 1)

            def ln_t1(b, par, k):
                high_part(made(b, "LN_T1", k)[0], h16[1], k).then_inc(s_hi1, 1)

            def q(b, par, p):
                bank, taken = made(b, "Q", p)
                op(qT[par][:, p, :], bank[:, 0:T], ACT.Identity, bias=bq_c[:, p:p + 1],
                   scale=post_q[:]).then_inc(taken, 1)

            def v(b, par, t):
                bank, taken = made(b, "V", t)
                op(vv[par][:, t, :], bank[:, 0:H], ACT.Copy, scale=VS).then_inc(taken, 1)

            def exp0(b, par, u):
                act.wait_ge(s_y0, n_s0.after(b, "QK0", u))
                if n_t.some_before(b, "PT0", u, 2):
                    act.wait_ge(s_t, n_t.before(b, "PT0", u, 2))
                for hh in range(2):
                    last = op(p0[:, u % 3, hh, :], y0[:, u % YB, hh, :], ACT.Exp, bias=min0[:, u, hh:hh + 1],
                              scale=-1.0, accum_out=sum0[:, u, hh:hh + 1])
                last.then_inc(s_e0, 1)

            def pt0(b, par, u):
                p, qt = divmod(u, 2)
                act.wait_ge(s_t, n_t.after(b, "PT0", u))
                op(pT0[:, p % 2, :, :, qt * P:(qt + 1) * P],
                   pt_ps[u % 2][:].rearrange("p (h k q) -> p h k q", h=2, k=NT), ACT.Copy).then_inc(s_pT, 1)

            def pv0(b, par, p):
                bank, _ = made(b, "PV0", p)
                op(c16[:, 0, p, :], bank[:, 0:T], ACT.Copy).then_inc(s_hi0, 1)

            def heads(b, par, t):
                bank, taken = made(b, "HEADS", t)
                if t == 0 and b.ref >= 1:
                    act.wait_ge(s_prod, n_prod.after(b.back(1), "SCORE_PROD"))
                op(th[:, t, :], bank[:, 0:H], ACT.Tanh, scale=post[:, WH:WH + 1]).then_inc(s_th, 1)
                op(hv[par][:, t, :], bank[:, 0:H], ACT.Copy, scale=post[:, WH:WH + 1]).then_inc(taken, 1)

            def gate_tanh(b, par, _):
                for t in range(NT):
                    _, _, taken, value = job(b, "GATE", t)
                    act.wait_ge(taken, value)
                if b.ref >= 1:
                    act.wait_ge(s_gate, n_gate.after(b.back(1), "GATES"))
                op(gtanh[:], gpre[:], ACT.Tanh, scale=0.5).then_inc(s_gtanh, 1)

            def dst(b, par, c):
                act.wait_ge(s_db, n_db.after(b, "DST", c))
                if n_y1.some_before(b, "LEAKY1", 2 * c, 2):
                    act.wait_ge(s_y1, n_y1.before(b, "LEAKY1", 2 * c, 2))
                op(dst5[:, c % 2].rearrange("p h t -> p (h t)"), unit_ps[c % 3][:], ACT.Copy,
                   scale=ALPHA).then_inc(s_d5, 1)

            def exp1(b, par, u):
                c, t = divmod(u, 2)
                act.wait_ge(s_y1, n_y1.after(b, "LEAKY1", u))
                if n_t.some_before(b, "PT1", u, 2):
                    act.wait_ge(s_t, n_t.before(b, "PT1", u, 2))
                if u == 0 and b.ref >= 1:
                    act.wait_ge(s_rec1, n_rec1.after(b.back(1), "RECIP1"))
                for hh in range(2):
                    h = 2 * c + hh
                    last = op(p1[:, u % 3, hh, :], y1[:, u % YB, hh, :], ACT.Exp, bias=min1[:, u, hh:hh + 1],
                              scale=-1.0, accum_out=sum1[:, t, h:h + 1])
                last.then_inc(s_e1, 1)

            def pt1(b, par, u):
                c, t = divmod(u, 2)
                g, q_ = divmod(2 * c, 4)
                act.wait_ge(s_t, n_t.after(b, "PT1", u))
                op(pT1[:, g % 2, q_:q_ + 2, :, t * P:(t + 1) * P],
                   pt_ps[u % 2][:].rearrange("p (h k q) -> p h k q", h=2, k=NT), ACT.Copy).then_inc(s_pT, 1)

            def pv1(b, par, g):
                bank, taken = made(b, "PV1", g)
                op(oT[:, g, :], bank[:, 0:T], ACT.Copy).then_inc(taken, 1)

            def elu_exp(b, par, _):
                act.wait_ge(s_ob, n_ob.after(b, "ELU_BIAS"))
                op(o1m[:], o1[:], ACT.Relu, scale=-1.0).then_inc(s_om, 1)
                act.wait_ge(s_om, n_om.after(b, "ELU_EXP"))
                op(o1m[:], o1m[:], ACT.Exp, scale=-1.0).then_inc(s_oe, 1)

            walk(act, {"LN_T0": ln_t0, "Q": q, "V": v, "EXP0": exp0, "PT0": pt0, "PV0": pv0, "LN_T1": ln_t1,
                       "HEADS": heads, "GATE_TANH": gate_tanh, "DST": dst, "EXP1": exp1, "PT1": pt1,
                       "PV1": pv1, "ELU_EXP": elu_exp})

        @block.vector
        def _(dve):
            chain = [0]

            def own(ins):
                chain[0] += 1
                ins.then_inc(s_setup, 1)
                dve.wait_ge(s_setup, chain[0])

            V = nc.vector
            dve.wait_ge(s_small, 16 * 8)
            for c in range(NC):
                last = V.tensor_copy(bv_w[:, c, :], bv_c[:, c:c + 1].broadcast_to([P, P]))
            last.then_inc(s_bvw, 1)
            own(V.tensor_scalar(bq_c[:], bq_c[:], -1.0 / 8.0, None, ALU.mult))
            own(V.tensor_scalar(src_row[:], src_row[:], -(1.0 - ALPHA), None, ALU.mult))
            own(V.tensor_scalar(dst_row[:], dst_row[:], -1.0, None, ALU.mult))
            for w in range(6):
                dve.wait_ge(s_w[w], 16)
                st = wstage[:, w % 2]
                own(V.scalar_tensor_tensor(wabs, st, -1.0, st, ALU.mult, ALU.max))
                own(V.reduce_max(wmax[:, w:w + 1], wabs.rearrange("p c n -> p (c n)"), AX_X))
                V.tensor_scalar(wmax[:, w:w + 1], wmax[:, w:w + 1], 1e-30, None, ALU.max).then_inc(s_wmax, 1)
                dve.wait_ge(s_wmax_all, w + 1)
                own(V.reciprocal(wscale[:, w:w + 1], wmax_all[:, w:w + 1]))
                own(V.tensor_scalar(wscale[:, w:w + 1], wscale[:, w:w + 1], WS, None, ALU.mult))
                own(V.reciprocal(post[:, w:w + 1], wscale[:, w:w + 1]))
                own(V.tensor_scalar(w16[:, w, 0], st, wscale[:, w:w + 1], None, ALU.mult))
                if w == WF:
                    dve.wait_ge(s_row, 1)
                    V.tensor_tensor(out0_row[:], job_ps[0][:, 0:H], out0_row[:], ALU.add).then_inc(s_rowdone, 1)
                V.scalar_tensor_tensor(w16[:, w, 1], st, wscale[:, w:w + 1], w16[:, w, 0],
                                       ALU.mult, ALU.subtract).then_inc(s_w16, 1)
            own(V.tensor_tensor(post_f[:], post[:, WV:WV + 1], post[:, WF:WF + 1], ALU.mult))
            own(V.tensor_scalar(post_f[:], post_f[:], 1.0 / (XS * VS), None, ALU.mult))
            own(V.tensor_scalar(post[:], post[:], 1.0 / XS, None, ALU.mult))
            own(V.tensor_scalar(post_q[:], post[:, WQ:WQ + 1], -1.0 / 8.0, None, ALU.mult))
            assert chain[0] == SETUP_SCALES

            def stats(src, k, step):
                def part(b, par, _):
                    if k == 0:
                        dve.wait_ge(s_x[par], loaded(b))
                    else:
                        for t in range(NT):
                            _, _, taken, value = job(b, "OUT0", t)
                            dve.wait_ge(taken, value)
                    for t in range(NT):
                        last = V.bn_stats(bn[:, t, :], (xb if k == 0 else x2)[par][:, t, :])
                    last.then_inc(s_bn, 1)
                    written = ready(dve, n_bn.after(b, step))
                    dve.wait_ge(s_pool_const, 8)
                    dve.wait_ge(s_bn, written)
                    for t in range(NT):
                        last = V.bn_aggr(mv[k][:, t, :], bn[:, t, :])
                    last.then_inc(s_mv, 1)
                return part

            def norm(src, k, step, rstep):
                def part(b, par, _):
                    dve.wait_ge(s_rstd, n_rstd.after(b, rstep))
                    for t in range(NT):
                        last = V.tensor_scalar(xn[k][:, t, :], (xb if k == 0 else x2)[par][:, t, :],
                                               mv[k][:, t, 0:1], rstd[k][:, t:t + 1], ALU.subtract, ALU.mult)
                    last.then_inc(s_norm, 1)
                return part

            def made(b, step, idx=0):
                bank, full, taken, value = job(b, step, idx)
                dve.wait_ge(full, value)
                return bank, taken

            def low_part(b, step, h, k):
                bank, _, taken, _ = job(b, step, k)
                c = slice(0, 2) if k == 0 else slice(2, 3)
                n = (c.stop - c.start) * T
                V.scalar_tensor_tensor(h[:, 1, c, :].rearrange("p c t -> p (c t)"), bank[:, 0:n], 0.0,
                                       h[:, 0, c, :].rearrange("p c t -> p (c t)"),
                                       ALU.max, ALU.subtract).then_inc(taken, 1)

            def ln_t0(b, par, k):
                dve.wait_ge(s_hi0, n_hi0.after(b, "LN_T0", k))
                low_part(b, "LN_T0", h16[0], k)

            def ln_t1(b, par, k):
                dve.wait_ge(s_hi1, n_hi1.after(b, "LN_T1", k))
                low_part(b, "LN_T1", h16[1], k)

            def k_(b, par, p):
                bank, taken = made(b, "K", p)
                for hh in range(2):
                    r = slice(D0 * hh, D0 * (hh + 1))
                    last = V.tensor_scalar(kz[par][r, 2 * p + hh, :], bank[r, 0:T], post[r, WK:WK + 1],
                                           bk_c[r, p:p + 1], ALU.mult, ALU.add)
                last.then_inc(taken, 1)

            def qk0(b, par, u):
                qt = u % 2
                masks = ready(dve, n_mask0.after(b, "MASK0"))
                scores = ready(dve, n_s0.after(b, "QK0", u))
                used = ready(dve, n_e0.before(b, "EXP0", u, YB - 1))
                dve.wait_ge(s_pool_const, 8)
                if u == 0:
                    dve.wait_ge(s_mask0, masks)
                dve.wait_ge(s_s0, scores)
                if n_e0.some_before(b, "EXP0", u, YB - 1):
                    dve.wait_ge(s_e0, used)
                for hh in range(2):
                    last = V.tensor_tensor_reduce(y0[:, u % YB, hh, :], unit_ps[u % 3][:, hh * T:(hh + 1) * T],
                                                  mask0[:, qt, :], 1.0, 3.0e38, ALU.add, ALU.min,
                                                  min0[:, u, hh:hh + 1])
                last.then_inc(s_y0, 1)

            def normp0(b, par, u):
                dve.wait_ge(s_e0, n_e0.after(b, "EXP0", u))
                V.reciprocal(rec0[:, u, :], sum0[:, u, :]).then_inc(s_rec0, 1)

            def pv0(b, par, p):
                dve.wait_ge(s_hi0, n_hi0.after(b, "PV0", p))
                bank, _, taken, _ = job(b, "PV0", p)
                V.tensor_tensor(c16[:, 1, p, :], bank[:, 0:T], c16[:, 0, p, :], ALU.subtract).then_inc(taken, 1)

            def out0(b, par, t):
                bank, taken = made(b, "OUT0", t)
                if t == 0:
                    dve.wait_ge(s_xc, n_xc.after(b, "RES_ROW"))
                    if b.ref >= 2:
                        dve.wait_ge(s_skip, n_skip.after(b.back(2), "SKIP"))
                V.scalar_tensor_tensor(x2[par][:, t, :], bank[:, 0:H], post_f[:], xc[:, t, :],
                                       ALU.mult, ALU.add).then_inc(taken, 1)

            def gate_proj(b, par, t):
                bank, taken = made(b, "GATE", t)
                if t == 0 and b.ref >= 1:
                    dve.wait_ge(s_gtanh, n_gtanh.after(b.back(1), "GATE_TANH"))
                V.scalar_tensor_tensor(gpre[:, t, :], bank[:, 0:H], post[:, WG:WG + 1], gate_b_row[:],
                                       ALU.mult, ALU.add).then_inc(taken, 1)

            def skip_h(b, par, _):
                dve.wait_ge(s_norm, n_norm.after(b, "NORM1"))
                if b.ref >= 1:
                    dve.wait_ge(s_ungate, n_ungate.after(b.back(1), "SKIP"))
                V.tensor_scalar(hskip[:], xn[1][:], 0.0, 1.0 / XS, ALU.max, ALU.mult).then_inc(s_hskip, 1)

            def score_sum(b, par, _):
                dve.wait_ge(s_prod, n_prod.after(b, "SCORE_PROD"))
                for i, dst_ in enumerate((s8[par], nd)):
                    V.reduce_sum(dst_[:].rearrange("p t h -> p (t h)"),
                                 prod[:, i].rearrange("p t (h e) -> p (t h) e", e=D1), AX_X).then_inc(s_sd, 1)
                dve.wait_ge(s_sd, n_sd.after(b, "SCORE_SUM", 0, 2))
                V.tensor_copy(nd_parts[:, :, 0, :], nd[:]).then_inc(s_sd, 1)
                dve.wait_ge(s_sd, n_sd.after(b, "SCORE_SUM", 0, 3))
                V.tensor_tensor(nd_r[:], nd[:], nd_parts[:, :, 0, :], ALU.subtract).then_inc(s_sd, 1)
                dve.wait_ge(s_sd, n_sd.after(b, "SCORE_SUM", 0, 4))
                V.tensor_copy(nd_parts[:, :, 1, :], nd_r[:]).then_inc(s_nd, 1)
                dve.wait_ge(s_nd, n_nd.after(b, "SCORE_SUM"))
                V.tensor_tensor(nd_parts[:, :, 2, :], nd_r[:], nd_parts[:, :, 1, :], ALU.subtract).then_inc(s_sd, 1)

            def dst_t(b, par, _):
                bank, taken = made(b, "DST_T")
                V.tensor_copy(ndT[par][0:3 * H1, :], bank[:].bitcast(BF16)[0:3 * H1, 0:T]).then_inc(taken, 1)

            def leaky1(b, par, u):
                c, t = divmod(u, 2)
                if u == 0:
                    dve.wait_ge(s_mask1, n_mask1.after(b, "MASK1"))
                if t == 0:
                    dve.wait_ge(s_d5, n_db.after(b, "DST", c))
                if n_e1.some_before(b, "EXP1", u, YB - 1):
                    dve.wait_ge(s_e1, n_e1.before(b, "EXP1", u, YB - 1))
                for hh in range(2):
                    h = 2 * c + hh
                    V.scalar_tensor_tensor(yw[:, u % 2, hh, :], unit_ps[c % 3][:, hh * T:(hh + 1) * T],
                                           s8[par][:, t, h:h + 1], dst5[:, c % 2, hh, :],
                                           ALU.add, ALU.min).then_inc(s_lk, 1)
                for hh in range(2):
                    written = ready(dve, n_lk.after(b, "LEAKY1", u, hh + 1))
                    dve.wait_ge(s_pool_const, 8)
                    dve.wait_ge(s_lk, written)
                    last = V.tensor_tensor_reduce(y1[:, u % YB, hh, :], yw[:, u % 2, hh, :], mask1[:, t, :],
                                                  1.0, 3.0e38, ALU.add, ALU.min, min1[:, u, hh:hh + 1])
                last.then_inc(s_y1, 1)

            def recip1(b, par, _):
                dve.wait_ge(s_e1, n_e1.after(b, "EXP1", 11))
                V.reciprocal(rec1[:].rearrange("p t h -> p (t h)"),
                             sum1[:].rearrange("p t h -> p (t h)")).then_inc(s_rec1, 1)

            def out_t(b, par, t):
                bank, taken = made(b, "OUT_T", t)
                if t == 0:
                    dve.wait_ge(s_rec1, n_rec1.after(b, "RECIP1"))
                V.tensor_tensor(o1[:, t, :].rearrange("p (h e) -> p h e", e=D1),
                                bank[:, 0:H].rearrange("p (h e) -> p h e", e=D1),
                                rec1[:, t, :].unsqueeze(2).broadcast_to([P, H1, D1]), ALU.mult).then_inc(taken, 1)

            def finish(b, par, k):
                if k == 0:
                    dve.wait_ge(s_oe, n_oe.after(b, "ELU_EXP"))
                    V.scalar_tensor_tensor(o1m[:], o1[:], 0.0, o1m[:], ALU.max, ALU.add).then_inc(s_fin, 1)
                else:
                    dve.wait_ge(s_fin, n_fin.after(b, "FINISH", 0))
                    if b.ref >= 1:
                        dve.wait_ge(s_out, n_out.after(b.back(1), "STORE"))
                    V.scalar_tensor_tensor(y[:], o1m[:], -1.0, gate[par][:], ALU.add, ALU.mult).then_inc(s_fin, 1)

            walk(dve, {"STATS0": stats(xb, 0, "STATS0"), "NORM0": norm(xb, 0, "NORM0", "RSTD0"), "LN_T0": ln_t0,
                       "K": k_, "QK0": qk0, "NORMP0": normp0, "PV0": pv0, "OUT0": out0,
                       "STATS1": stats(x2, 1, "STATS1"), "NORM1": norm(x2, 1, "NORM1", "RSTD1"), "LN_T1": ln_t1,
                       "GATE": gate_proj, "SCORE_SUM": score_sum, "DST_T": dst_t, "LEAKY1": leaky1,
                       "RECIP1": recip1, "OUT_T": out_t, "FINISH": finish, "SKIP_H": skip_h})

        @block.gpsimd
        def _(pool):
            G = nc.gpsimd
            G.memset(ident[:], 0.0).then_inc(s_pool_const, 1)
            G.memset(pick[:], 0.0).then_inc(s_pool_const, 1)
            G.memset(half[:], -0.5).then_inc(s_pool_const, 1)
            pool.wait_ge(s_pool_const, 3)
            G.affine_select(out=ident[:], in_=ident[:], compare_op=ALU.not_equal, fill=1.0, base=0,
                            pattern=[[-1, P]], channel_multiplier=1).then_inc(s_pool_const, 1)
            for i in range(3):
                G.affine_select(out=pick[:], in_=pick[:], compare_op=ALU.not_equal, fill=1.0, base=-H1 * i,
                                pattern=[[-1, H1], [0, P]], channel_multiplier=1).then_inc(s_pool_const, 1)
                pool.wait_ge(s_pool_const, 5 + i)
            for i in range(2):
                G.memset(kz[i][:], 0.0)
                G.memset(ndT[i][:], 0.0)
            G.tensor_copy(ident_b[:], ident[:]).then_inc(s_pool_const, 1)
            for w in range(6):
                pool.wait_ge(s_wmax, w + 1)
                G.partition_all_reduce(wmax_all[:, w:w + 1], wmax[:, w:w + 1], P, RMAX).then_inc(s_wmax_all, 1)

            def mask0_(b, par, _):
                here = ready(pool, loaded(b))
                read = ready(pool, n_s0.after(b.back(1), "QK0", 5)) if b.ref >= 1 else None
                pool.wait_ge(s_pool_const, 8)
                pool.wait_ge(s_adj[par], here)
                if b.ref >= 1:
                    pool.wait_ge(s_y0, read)
                G.tensor_scalar(mask0[:], adj_raw[par][:], -1.0, -BIG, ALU.add, ALU.mult).then_inc(s_mask0, 1)

            def mask1_(b, par, _):
                here = ready(pool, loaded(b))
                read = ready(pool, n_y1.after(b.back(1), "LEAKY1", 11)) if b.ref >= 1 else None
                pool.wait_ge(s_pool_const, 8)
                pool.wait_ge(s_adj[par], here)
                if b.ref >= 1:
                    pool.wait_ge(s_y1, read)
                G.tensor_scalar(mask1[:], adj_raw[par][:], -1.0, -BIG, ALU.add, ALU.mult).then_inc(s_mask1, 1)

            def rstd_(k, step, sstep):
                def part(b, par, _):
                    here = ready(pool, n_mv.after(b, sstep))
                    pool.wait_ge(s_pool_const, 8)
                    pool.wait_ge(s_mv, here)
                    G.tensor_scalar(veps[:, k, :], mv[k][:, :, 1], EPS, XS ** -2, ALU.add, ALU.mult).then_inc(s_veps, 1)
                    pool.wait_ge(s_veps, n_veps.after(b, step))
                    G.tensor_tensor(rstd[k][:], veps[:, k, :], half[:], ALU.pow).then_inc(s_rstd, 1)
                return part

            def normp0(b, par, u):
                here = ready(pool, n_np0.after(b, "NORMP0", u))
                pool.wait_ge(s_pool_const, 8)
                pool.wait_ge(s_rec0, here)
                for hh in range(2):
                    last = G.tensor_scalar(p0[:, u % 3, hh, :], p0[:, u % 3, hh, :], rec0[:, u, hh:hh + 1], 1.0,
                                           ALU.mult, ALU.mult)
                last.then_inc(s_p0, 1)

            def res_row(b, par, _):
                pool.wait_ge(s_x[par], loaded(b))
                if b.ref == 0:
                    pool.wait_ge(s_rowdone, 1)
                else:
                    for t in range(NT):
                        _, _, taken, value = job(b.back(1), "OUT0", t)
                        pool.wait_ge(taken, value)
                G.tensor_tensor(xc[:], xb[par][:], out0_row[:].unsqueeze(1).broadcast_to([P, NT, H]),
                                ALU.add).then_inc(s_xc, 1)

            def score_prod(b, par, _):
                pool.wait_ge(s_th, n_th.after(b, "HEADS", 1))
                if b.ref >= 1:
                    pool.wait_ge(s_sd, n_sd.after(b.back(1), "SCORE_SUM"))
                else:
                    pool.wait_ge(s_setup, 3)
                for i, row in enumerate((src_row, dst_row)):
                    last = G.tensor_tensor(prod[:, i], th[:], row[:].unsqueeze(1).broadcast_to([P, NT, H]), ALU.mult)
                last.then_inc(s_prod, 1)

            def gates(b, par, _):
                tanh = ready(pool, n_gtanh.after(b, "GATE_TANH"))
                used = ready(pool, n_fin.after(b.back(2), "FINISH", 1)) if b.ref >= 2 else None
                pool.wait_ge(s_pool_const, 8)
                pool.wait_ge(s_gtanh, tanh)
                if b.ref >= 2:
                    pool.wait_ge(s_fin, used)
                G.tensor_scalar(gate[par][:], gtanh[:], 0.5, 0.5, ALU.mult, ALU.add)
                G.tensor_scalar(ungate[:], gtanh[:], -0.5, 0.5, ALU.mult, ALU.add).then_inc(s_gate, 1)

            def skip(b, par, _):
                pool.wait_ge(s_gate, n_gate.after(b, "GATES"))
                pool.wait_ge(s_hskip, n_hskip.after(b, "SKIP_H"))
                G.tensor_tensor(ungate[:], ungate[:], hskip[:], ALU.mult).then_inc(s_ungate, 1)
                pool.wait_ge(s_ungate, n_ungate.after(b, "SKIP"))
                G.tensor_tensor(xskip[par][:], ungate[:], x2[par][:], ALU.add).then_inc(s_skip, 1)

            def elu_bias(b, par, _):
                for t in range(NT):
                    _, _, taken, value = job(b, "OUT_T", t)
                    pool.wait_ge(taken, value)
                G.tensor_tensor(o1[:].rearrange("p t (h e) -> p (t h) e", e=D1),
                                o1[:].rearrange("p t (h e) -> p (t h) e", e=D1),
                                gat_b_row[:].unsqueeze(1).broadcast_to([P, NT * H1, D1]), ALU.add).then_inc(s_ob, 1)

            def out_sum(b, par, _):
                pool.wait_ge(s_fin, n_fin.after(b, "FINISH", 1))
                G.tensor_tensor(y[:], y[:], xskip[par][:], ALU.add).then_inc(s_sum, 1)

            walk(pool, {"MASK0": mask0_, "MASK1": mask1_, "RSTD0": rstd_(0, "RSTD0", "STATS0"), "RSTD1": rstd_(1, "RSTD1", "STATS1"),
                        "NORMP0": normp0, "RES_ROW": res_row, "SCORE_PROD": score_prod, "GATES": gates, "SKIP": skip,
                        "ELU_BIAS": elu_bias, "OUT_SUM": out_sum})


SETUP_SCALES = 3 + 6 * 6 + 4

_INS = ["x", "adj", "w_all", "bq", "bk", "bv", "bf", "gat_b", "w_src", "w_dst", "gate_b"]


def kernel(x, adj, L0_gnn_Wq, L0_gnn_bq, L0_gnn_Wk, L0_gnn_bk, L0_gnn_Wv, L0_gnn_bv, L0_gnn_Wf, L0_gnn_bf,
           L1_gnn_W, L1_gnn_b, L1_gnn_w_src, L1_gnn_w_dst, L1_gnn_H_w, L1_gnn_H_b):
    import concourse.bacc as bacc
    from concourse.bass_utils import run_bass_kernel_spmd

    heads_w = np.asarray(L1_gnn_W).transpose(1, 0, 2).reshape(H, H)


    def columns(a):
        return np.asarray(a).reshape(NC, P).T

    given = {
        "x": x, "adj": adj,
        "w_all": np.stack([np.asarray(L0_gnn_Wq), np.asarray(L0_gnn_Wk), np.asarray(L0_gnn_Wv),
                           np.asarray(L0_gnn_Wf), heads_w, np.asarray(L1_gnn_H_w).T]),
        "bq": columns(L0_gnn_bq), "bk": columns(L0_gnn_bk), "bv": columns(L0_gnn_bv), "bf": L0_gnn_bf, "gat_b": L1_gnn_b,
        "w_src": np.asarray(L1_gnn_w_src).reshape(H), "w_dst": np.asarray(L1_gnn_w_dst).reshape(H),
        "gate_b": L1_gnn_H_b,
    }
    nc = bacc.Bacc("TRN2", target_bir_lowering=False, num_devices=1)
    arrays, args = {}, []
    for name in _INS:
        a = np.ascontiguousarray(given[name])
        arrays[f"in_{name}_dram"] = a
        args.append(nc.dram_tensor(f"in_{name}_dram", a.shape, mybir.dt.from_np(a.dtype), kind="ExternalInput").ap())
    out = nc.dram_tensor("out_dram", np.asarray(x).shape, F32, kind="ExternalOutput").ap()
    build(nc, *args, out)
    r = run_bass_kernel_spmd(nc, [arrays], core_ids=[0])
    return r.results[0]["out_dram"]
```

```python
from contextlib import ExitStack

import numpy as np

import concourse.bass as bass
from concourse import mybir

F32, F16, BF16, U8 = mybir.dt.float32, mybir.dt.float16, mybir.dt.bfloat16, mybir.dt.uint8
ALU = mybir.AluOpType
ACT = mybir.ActivationFunctionType
AX_X = mybir.AxisListType.X
RMAX = bass.bass_isa.ReduceOp.max

P = 128
T = 256
H = 384
NT = T // P
NC = H // P
H0, D0 = 6, 64
H1, D1 = 12, 32
BIG = 9.0e15
ALPHA = 0.2
EPS = 1e-5
XS = 1024.0
WS = 16384.0
VS = 2.0 ** -16
WQ, WK, WF, WV, WH, WG = range(6)
YB = 3
TERMS = ((0, 0), (0, 1), (1, 0))


FILL = {
    0: [("C", "RECIP1", 0), ("B", "GATE", 0), ("P", "RSTD0", 0), ("P", "NORM0", 0)],
    1: [],
    2: [("B", "SCORE_SUM", 0), ("B", "GATE", 1), ("C", "PV1", 2), ("B", "DST_T", 0)],
    3: [("P", "LN_T0", 0)],
    4: [("C", "OUT_T", 0), ("B", "SKIP_H", 0), ("B", "MASK1", 0), ("P", "LN_T0", 1)],
    5: [("A", "PV0", 0), ("C", "OUT_T", 1), ("P", "MASK0", 0), ("P", "Q", 0)],
    6: [("P", "K", 0), ("A", "PV0", 1), ("P", "LOAD_ADJ", 0), ("C", "ELU_BIAS", 0)],
    7: [("P", "K", 1), ("C", "ELU_RELU", 0), ("C", "ELU_EXP", 0)],
    8: [("B", "GATES", 0), ("P", "Q", 1), ("A", "PV0", 2), ("P", "Q", 2), ("A", "RES_ROW", 0)],
    9: [("C", "FINISH", 0), ("C", "FINISH", 1)],
    10: [("A", "OUT0", 0), ("C", "OUT_SUM", 0), ("A", "OUT0", 1)],
    11: [("P", "V", 0)],
    12: [("A", "STATS1", 0), ("A", "STATS1", 1), ("A", "AGGREGATE1", 0)],
    13: [("P", "V", 1), ("L", "LOAD_X", 0), ("A", "LN_T1", 0), ("A", "LN_T1", 1), ("A", "NORM1", 0)],
    14: [("B", "PV1", 0), ("A", "RSTD1", 0), ("C", "STORE", 0), ("P", "K", 2)],
    15: [("A", "HEADS", 0)],
    16: [("B", "SKIP", 0), ("A", "HEADS", 1)],
    17: [("A", "SCORE_PROD", 0), ("L", "STATS0", 0), ("B", "PV1", 1)],
}
JOBS = {"LN_T0": 1, "Q": 1, "K": 1, "V": 1, "PV0": 1, "OUT0": 1, "LN_T1": 1, "HEADS": 1, "GATE": 1,
        "DST_T": 1, "PV1": 1, "OUT_T": 1}
LATER = {"L": "P", "P": "A", "A": "B", "B": "C", "C": "D"}


UNITS = [("A", u) for u in range(6)] + [("B", u) for u in range(12)]
SEQUENCE = {
    "PE": ("DST", "SCORES", "PT", "MAKE"),
    "ACT": ("TAKE", "DST", "PT", "EXP", "REST"),
    "DVE": ("NORMP", "REST", "TAKE", "SCORES"),
    "POOL": ("NORMP", "REST"),
    "SP": ("REST",),
}


def order_of_steps(sequence):
    n = len(UNITS)

    def attention(slot, step):
        ph, u = UNITS[slot % n]
        return [(ph if slot >= 0 else LATER[ph], step + ("0" if ph == "A" else "1"), u)]

    def jobs(slot):
        return [(ph if slot >= 0 else LATER[ph], step, idx) for ph, step, idx in FILL[slot % n] if step in JOBS]

    steps = []
    for slot in range(n):
        for what in sequence:
            if what == "PT":
                steps += attention(slot - 3, "PT")
            elif what == "EXP":
                steps += attention(slot - 1, "EXP")
            elif what == "NORMP" and UNITS[slot - 2][0] == "A":
                steps += attention(slot - 2, "NORMP")
            elif what == "SCORES":
                steps += attention(slot, "SCORES")
            elif what == "DST" and slot + 1 < n and UNITS[slot + 1][0] == "B" and UNITS[slot + 1][1] % 2 == 0:
                steps.append(("B", "DST", UNITS[slot + 1][1] // 2))
            elif what == "MAKE":
                steps += jobs(slot)
            elif what == "TAKE":
                steps += jobs(slot - 1)
            elif what == "REST":
                steps += [step for step in FILL[slot] if step[1] not in JOBS]
    return steps


ORDERS = {engine: order_of_steps(sequence) for engine, sequence in SEQUENCE.items()}
ORDER = order_of_steps(("PT", "DST", "NORMP", "EXP", "SCORES", "MAKE", "REST"))
LAG = {"L": -2, "P": -1, "A": 0, "B": 1, "C": 2, "D": 3}


class Batch:

    def __init__(self, ref, reg=None):
        self.ref, self.reg = ref, reg

    def back(self, k):
        return Batch(self.ref - k, self.reg)

    def value(self):
        return self.ref if self.reg is None else self.reg * 2 + self.ref


class Count:

    def __init__(self, n_batch, per_step, unit=1):
        self.per_step, self.unit, self.n = per_step, unit, n_batch
        self.starts = {-2: 0}
        for it in range(-2, n_batch + 3):
            self.starts[it + 1] = self.starts[it] + sum(per_step[s] for ph, s, _ in ORDER if self._on(ph, it, s))
        self.per = self.starts[5] - self.starts[4]

    def _on(self, phase, it, step):
        return step in self.per_step and 0 <= it - LAG[phase] < self.n

    def _ahead(self, batch, step, idx):
        assert 0 <= batch.ref < self.n, (step, batch.ref)
        it = batch.ref + next(LAG[ph] for ph, s, i in ORDER if (s, i) == (step, idx))
        n = self.starts[it]
        for ph, s, i in ORDER:
            if (s, i) == (step, idx):
                return n
            if self._on(ph, it, s):
                n += self.per_step[s]

    def _value(self, batch, n):
        v = n * self.unit
        return v if batch.reg is None else batch.reg * (2 * self.per * self.unit) + v

    def before(self, batch, step, idx=0, less=0):
        return self._value(batch, self._ahead(batch, step, idx) - less)

    def some_before(self, batch, step, idx=0, less=0):
        return self._ahead(batch, step, idx) - less > 0

    def after(self, batch, step, idx=0, k=None):
        return self._value(batch, self._ahead(batch, step, idx) + (self.per_step[step] if k is None else k))


class Jobs(Count):
    BANKS = 3

    def __init__(self, n_batch):
        super().__init__(n_batch, JOBS)
        assert 2 * self.per % self.BANKS == 0

    def bank(self, batch, step, idx):
        return self._ahead(batch, step, idx) % self.BANKS

    def used(self, batch, step, idx):
        return self._ahead(batch, step, idx) >= self.BANKS

    def before(self, batch, step, idx=0):
        v = self._ahead(batch, step, idx) // self.BANKS
        return v if batch.reg is None else batch.reg * (2 * self.per // self.BANKS) + v

    def after(self, batch, step, idx=0):
        return self.before(batch, step, idx) + 1


def build(nc, x, adj, w_all, bq, bk, bv, bf, gat_b, w_src, w_dst, gate_b, out):
    NB = x.shape[0]
    LOOP = (NB - 6) // 2
    assert NB % 2 == 0 and LOOP >= 1

    x_v = x.rearrange("b (t p) h -> b p t h", p=P)
    out_v = out.rearrange("b (t p) h -> b p t h", p=P)
    adj_v = adj.rearrange("b (t p) m -> b p t m", p=P)
    w_v = w_all.rearrange("w (c p) n -> w p c n", p=P)

    with ExitStack() as ctx:
        def sb(name, shape, dt=F32):
            return ctx.enter_context(nc.sbuf_tensor(name, shape, dt))

        def sem(name):
            return ctx.enter_context(nc.semaphore(name))

        def banks(name, n):
            return [ctx.enter_context(nc.psum_tensor(f"{name}{i}", [P, 512], F32)) for i in range(n)]

        job_ps = banks("job", Jobs.BANKS)
        unit_ps = banks("unit", 3)
        pt_ps = banks("pt", 2)

        w16 = sb("w16", [P, 6, 2, NC, H], F16)
        wsum = sb("wsum", [P, 6])
        wsum_all = sb("wsum_all", [P, 6])
        wscale = sb("wscale", [P, 6])
        post = sb("post", [P, 6])
        post_q = sb("post_q", [P, 1])
        post_g = sb("post_g", [P, 1])
        post_f = sb("post_f", [P, 1])
        bq_c = sb("bq_c", [P, NC])
        bk_c = sb("bk_c", [P, NC])
        bv_c = sb("bv_c", [P, NC])
        bv_w = sb("bv_w", [P, NC, P])
        out0_row = sb("out0_row", [P, H])
        gat_b_row = sb("gat_b_row", [P, D1])
        gate_b_row = sb("gate_b_row", [P, H])
        src_row = sb("src_row", [P, H])
        dst_row = sb("dst_row", [P, H])
        ident = sb("ident", [P, P])
        ident_b = sb("ident_b", [P, P], BF16)
        pick = sb("pick", [P, H1, P], BF16)
        half = sb("half", [P, NT])

        xb = [sb(f"xb{i}", [P, NT, H]) for i in range(2)]
        adj_raw = [sb(f"adj_raw{i}", [P, NT, T], U8) for i in range(2)]
        mask0 = sb("mask0", [P, NT, T])
        mask1 = sb("mask1", [P, NT, T])
        bn = [sb(f"bn{i}", [P, NT, 6]) for i in range(2)]
        mv = [sb(f"mv{i}", [P, NT, 2]) for i in range(2)]
        nmean = sb("nmean", [P, NT])
        veps = sb("veps", [P, 2, NT])
        rstd = [sb(f"rstd{i}", [P, NT]) for i in range(2)]
        xn = [sb(f"xn{i}", [P, NT, H]) for i in range(2)]
        h16 = [sb(f"h16_{i}", [P, 2, NC, T], F16) for i in range(2)]
        qT = [sb(f"qT{i}", [P, 3, T]) for i in range(2)]
        kz = [sb(f"kz{i}", [P, H0, T]) for i in range(2)]
        vv = [sb(f"vv{i}", [P, NT, H]) for i in range(2)]
        y0 = sb("y0", [P, YB, 2, T])
        p0 = sb("p0", [P, 3, 2, T])
        min0 = sb("min0", [P, 6, 2])
        sum0 = sb("sum0", [P, 6, 2])
        rec0 = sb("rec0", [P, 6, 2])
        pT0 = sb("pT0", [P, 2, 2, NT, T])
        c16 = sb("c16", [P, 2, 3, T], F16)
        xc = sb("xc", [P, NT, H])
        x2 = [sb(f"x2_{i}", [P, NT, H]) for i in range(2)]
        th = sb("th", [P, NT, H])
        prod = sb("prod", [P, 2, NT, H])
        hv = [sb(f"hv{i}", [P, NT, H]) for i in range(2)]
        s8 = [sb(f"s8_{i}", [P, NT, H1]) for i in range(2)]
        nd = sb("nd", [P, NT, H1])
        nd_r = sb("nd_r", [P, NT, H1])
        nd_parts = sb("nd_parts", [P, NT, 3, H1], BF16)
        ndT = [sb(f"ndT{i}", [P, T], BF16) for i in range(2)]
        ones_b = sb("ones_b", [P, P], BF16)
        gate_b3 = sb("gate_b3", [P, H], BF16)
        gate_part = sb("gate_part", [P, H], BF16)
        gtanh = sb("gtanh", [P, NT, H])
        gate = [sb(f"gate{i}", [P, NT, H]) for i in range(2)]
        ungate = sb("ungate", [P, NT, H])
        hskip = sb("hskip", [P, NT, H])
        xskip = [sb(f"xskip{i}", [P, NT, H]) for i in range(2)]
        dst5 = sb("dst5", [P, 2, 2, T])
        yw = sb("yw", [P, 2, 2, T])
        y1 = sb("y1", [P, YB, 2, T])
        p1 = sb("p1", [P, 3, 2, T])
        min1 = sb("min1", [P, 12, 2])
        sum1 = sb("sum1", [P, NT, H1])
        rec1 = sb("rec1", [P, NT, H1])
        pT1 = sb("pT1", [P, 2, 4, NT, T])
        def room(tensor, names, n=1):
            flat = tensor[:].rearrange(f"p {names} -> p ({names})")
            return [flat[:, i * NC * H:(i + 1) * NC * H].rearrange("p (c n) -> p c n", c=NC) for i in range(n)]

        stage = (room(pT0, "a h k t") + room(prod, "i t h") + room(p1, "a h t")
                 + room(pT1, "a q k t", 3))
        assert WV == 3
        stage[WF], stage[WV] = stage[3], stage[2]
        wabs = room(y1, "a h t")[0]
        oT = sb("oT", [P, 3, T])
        o1 = sb("o1", [P, NT, H])
        o1m = sb("o1m", [P, NT, H])
        y = sb("y", [P, NT, H])

        s_w = [sem(f"s_weight{i}") for i in range(6)]
        s_small = sem("s_small_inputs")
        s_wsum = sem("s_weight_sums")
        s_high = sem("s_weight_high_part")
        s_wsum_all = sem("s_wsum_all")
        s_w16 = sem("s_w16")
        s_setup = sem("s_setup_dve")
        s_pool_const = sem("s_pool_const")
        s_bvw = sem("s_bvw")
        s_row = sem("s_row")
        s_rowdone = sem("s_rowdone")

        s_x = [sem(f"s_x_loaded{i}") for i in range(2)]
        s_adj = [sem(f"s_adj_loaded{i}") for i in range(2)]
        n_job = Jobs(NB)
        s_full = [sem(f"s_job_made{i}") for i in range(Jobs.BANKS)]
        s_done = [sem(f"s_job_taken{i}") for i in range(Jobs.BANKS)]
        s_mask0, n_mask0 = sem("s_mask0"), Count(NB, {"MASK0": 1})
        s_mask1, n_mask1 = sem("s_mask1"), Count(NB, {"MASK1": 1})
        s_bn, n_bn = sem("s_bn_stats"), Count(NB, {"STATS0": 1, "STATS1": 1})
        s_mv, n_mv = sem("s_mean_var"), Count(NB, {"STATS0": 1, "AGGREGATE1": 1})
        s_veps, n_veps = sem("s_veps"), Count(NB, {"RSTD0": 1, "RSTD1": 1})
        s_rstd, n_rstd = sem("s_rstd"), Count(NB, {"RSTD0": 1, "RSTD1": 1})
        s_norm0, n_norm0 = sem("s_normalised0"), Count(NB, {"NORM0": 1})
        s_norm1, n_norm1 = sem("s_normalised1"), Count(NB, {"NORM1": 1})
        s_q, n_q = sem("s_q_in_sbuf"), Count(NB, {"Q": 1})
        s_hi0, n_hi0 = sem("s_high_part0"), Count(NB, {"LN_T0": 1, "PV0": 1})
        s_hi1, n_hi1 = sem("s_high_part1"), Count(NB, {"LN_T1": 1})
        s_s0, n_s0 = sem("s_scores0"), Count(NB, {"SCORES0": 1})
        s_y0 = sem("s_masked0")
        s_e0, n_e0 = sem("s_exp0"), Count(NB, {"EXP0": 1})
        s_rec0, n_np0 = sem("s_reciprocal0"), Count(NB, {"NORMP0": 1})
        s_p0 = sem("s_probs0")
        s_t, n_t = sem("s_probs_transposed"), Count(NB, {"PT0": 1, "PT1": 1})
        s_pT = sem("s_pT_in_sbuf")
        s_xc, n_xc = sem("s_residual_row"), Count(NB, {"RES_ROW": 1})
        s_th, n_th = sem("s_tanh_heads"), Count(NB, {"HEADS": 1})
        s_prod, n_prod = sem("s_score_products"), Count(NB, {"SCORE_PROD": 1})
        s_halves, n_halves = sem("s_score_halves_added"), Count(NB, {"SCORE_PROD": 1})
        s_sd, n_sd = sem("s_score_parts"), Count(NB, {"SCORE_SUM": 5})
        s_nd, n_nd = sem("s_dst_middle_part"), Count(NB, {"SCORE_SUM": 1})
        s_gate_b = sem("s_gate_bias_parts")
        s_hskip, n_hskip = sem("s_skip_h"), Count(NB, {"SKIP_H": 1})
        s_gate, n_gate = sem("s_gates"), Count(NB, {"GATES": 1})
        s_ungate, n_ungate = sem("s_ungated_h"), Count(NB, {"SKIP": 1})
        s_skip, n_skip = sem("s_skip"), Count(NB, {"SKIP": 1})
        s_db, n_db = sem("s_dst_rows"), Count(NB, {"DST": 1})
        s_d5 = sem("s_dst_rows_scaled")
        s_lk, n_lk = sem("s_leaky"), Count(NB, {"SCORES1": 2})
        s_y1, n_y1 = sem("s_masked1"), Count(NB, {"SCORES1": 1})
        s_e1, n_e1 = sem("s_exp1"), Count(NB, {"EXP1": 1})
        s_rec1, n_rec1 = sem("s_reciprocal1"), Count(NB, {"RECIP1": 1})
        s_ob, n_ob = sem("s_elu_bias"), Count(NB, {"ELU_BIAS": 1})
        s_om, n_om = sem("s_elu_negative"), Count(NB, {"ELU_RELU": 1})
        s_oe, n_oe = sem("s_elu_exp"), Count(NB, {"ELU_EXP": 1})
        s_fin, n_fin = sem("s_finish"), Count(NB, {"FINISH": 1})
        s_sum, n_sum = sem("s_output_rows"), Count(NB, {"OUT_SUM": 1})
        s_out, n_out = sem("s_stored"), Count(NB, {"STORE": 1}, 16)

        def ready(eng, value):
            if isinstance(value, int):
                return value
            if eng.engine not in count_regs:
                count_regs[eng.engine] = [eng.alloc_register(f"count{i}_{eng.engine.name}") for i in range(3)]
            regs = count_regs[eng.engine]
            regs.append(regs.pop(0))
            eng.reg_mov(regs[-1], value)
            return regs[-1]

        count_regs = {}

        def loaded(b):
            v = 16 * (b.ref // 2 + 1)
            return v if b.reg is None else b.reg * 16 + v

        def job(b, step, idx=0):
            i = n_job.bank(b, step, idx)
            return job_ps[i], s_full[i], s_done[i], n_job.after(b, step, idx)

        def walk(eng, order, parts, after={}):
            def iteration(it, reg=None):
                for phase, step, idx in order:
                    b = Batch(it - LAG[phase], reg)
                    if step in parts and 0 <= b.ref < NB:
                        parts[step](b, b.ref % 2, idx)
            for n in range(-2, 4):
                iteration(n)
                if n in after:
                    after[n]()
            with eng.Fori(0, LOOP) as j:
                iteration(4, j)
                iteration(5, j)
            for n in range(NB - 2, NB + 3):
                iteration(n)

        block = ctx.enter_context(nc.Block())

        @block.sync
        def _(sp):
            small = [
                (bv_c[:], bv), (bq_c[:], bq), (bk_c[:], bk),
                (out0_row[:], bf.partition_broadcast(P)), (gat_b_row[:], gat_b.partition_broadcast(P)),
                (gate_b_row[:], gate_b.partition_broadcast(P)), (src_row[:], w_src.partition_broadcast(P)),
                (dst_row[:], w_dst.partition_broadcast(P)),
            ]

            def load_weight(w):
                sp.dma_start(stage[w], w_v[w]).then_inc(s_w[w], 16)

            def load_others():
                for dst, src in small:
                    sp.dma_start(dst, src).then_inc(s_small, 16)
                for w in (WF, WV, WH, WG):
                    load_weight(w)

            load_weight(WQ)
            load_weight(WK)

            def of_batch(view, b, rows):
                return view[b.value()] if b.reg is None else view[bass.ds(b.value(), 1)].rearrange(rows)

            def load_x(b, par, _):
                x_b = of_batch(x_v, b, "a p t h -> (a p) t h")
                if b.ref >= 2:
                    sp.wait_ge(s_norm0, n_norm0.after(b.back(2), "NORM0"))
                    sp.wait_ge(s_xc, n_xc.after(b.back(2), "RES_ROW"))
                sp.dma_start(xb[par][:], x_b).then_inc(s_x[par], 16)

            def load_adj(b, par, _):
                adj_b = of_batch(adj_v, b, "a p t m -> (a p) t m")
                if b.ref >= 2:
                    used = ready(sp, n_mask1.after(b.back(2), "MASK1"))
                    sp.wait_ge(s_pool_const, 8)
                    sp.wait_ge(s_mask1, used)
                sp.dma_start(adj_raw[par][:], adj_b).then_inc(s_adj[par], 16)

            def store(b, par, _):
                out_b = of_batch(out_v, b, "a p t h -> (a p) t h")
                sp.wait_ge(s_sum, n_sum.after(b, "OUT_SUM"))
                sp.dma_start(out_b, y[:]).then_inc(s_out, 16)

            walk(sp, ORDERS["SP"], {"LOAD_X": load_x, "LOAD_ADJ": load_adj, "STORE": store}, {-2: load_others})
            sp.wait_ge(s_out, 16 * NB)

        @block.tensor
        def _(pe):
            mm = nc.tensor.matmul

            pe.wait_ge(s_w[WF], 16)
            pe.wait_ge(s_bvw, 1)
            for c in range(NC):
                last = mm(pt_ps[0][:, 0:H], bv_w[:, c, :], stage[WF][:, c, :], start=c == 0, stop=c == NC - 1)
            last.then_inc(s_row, 1)
            pe.wait_ge(s_pool_const, 8)

            def first_use(b, idx, w):
                if b.ref == 0 and idx == 0:
                    pe.wait_ge(s_w16, w + 1)

            def bank_free(b, step, idx, needs=()):
                bank, made, taken, _ = job(b, step, idx)
                wait_taken(b, needs, n_job.bank(b, step, idx))
                if n_job.used(b, step, idx):
                    pe.wait_ge(taken, n_job.before(b, step, idx))
                return bank, made

            def wait_taken(b, needs, but=None):
                last = {n_job.bank(b, step, idx): (step, idx) for step, idx in needs}
                for bank, (step, idx) in last.items():
                    if bank != but:
                        pe.wait_ge(s_done[bank], n_job.after(b, step, idx))

            def transpose_norm(bank, src, k):
                for i, c in enumerate((0, 1) if k == 0 else (2,)):
                    for t in range(NT):
                        last = nc.tensor.transpose(bank[:, i * T + t * P:i * T + (t + 1) * P],
                                                   src[:, t, c * P:(c + 1) * P], ident[:])
                return last

            def to_rows(bank, rows, t, w, bias=False):
                n = 0
                if bias:
                    mm(bank[:, 0:H], ones_b[:], gate_b3[:], start=True, stop=False)
                    n = 1
                for c in range(NC):
                    for i, j in TERMS:
                        last = mm(bank[:, 0:H], rows[:, i, c, t * P:(t + 1) * P], w16[:, w, j, c, :],
                                  start=n == 0, stop=(c, i, j) == (NC - 1, *TERMS[-1]))
                        n += 1
                return last

            def to_columns(step, w):
                def part(b, par, p):
                    first_use(b, p, w)
                    bank, made = bank_free(b, step, p, (("LN_T0", 0), ("LN_T0", 1)) if (step, p) == ("Q", 0) else ())
                    n = 0
                    for c in range(NC):
                        for i, j in TERMS:
                            last = mm(bank[:, 0:T], w16[:, w, i, c, p * P:(p + 1) * P], h16[0][:, j, c, :],
                                      start=n == 0, stop=n == 3 * NC - 1)
                            n += 1
                    last.then_inc(made, 1)
                return part

            def ln_t0(b, par, k):
                if k == 0:
                    pe.wait_ge(s_norm0, n_norm0.after(b, "NORM0"))
                bank, made = bank_free(b, "LN_T0", k)
                transpose_norm(bank, xn[0], k).then_inc(made, 1)

            def v(b, par, t):
                first_use(b, t, WV)
                bank, made = bank_free(b, "V", t)
                to_rows(bank, h16[0], t, WV).then_inc(made, 1)

            def qk0(b, par, u):
                p, qt = divmod(u, 2)
                if qt == 0:
                    wait_taken(b, (("Q", p), ("K", p)))
                if u >= 3:
                    pe.wait_ge(s_y0, n_s0.after(b, "SCORES0", u - 3))
                elif b.ref >= 2:
                    pe.wait_ge(s_y1, n_y1.after(b.back(2), "SCORES1", 2 * u + 7))
                elif b.ref == 1:
                    pe.wait_ge(s_y0, n_s0.after(b.back(1), "SCORES0", u + 3))
                mm(unit_ps[u % 3][:], qT[par][:, p, qt * P:(qt + 1) * P], kz[par][:, 2 * p:2 * p + 2, :],
                   start=True, stop=True).then_inc(s_s0, 1)

            def dst(b, par, c):
                if c == 0:
                    wait_taken(b, (("DST_T", 0),))
                if c >= 3:
                    pe.wait_ge(s_y1, n_y1.after(b, "SCORES1", 2 * c - 5))
                elif b.ref + 1 < NB:
                    pe.wait_ge(s_y0, n_s0.after(b.back(-1), "SCORES0", c + 3))
                else:
                    pe.wait_ge(s_y1, n_y1.after(b.back(1), "SCORES1", 2 * c + 7))
                for hh in range(2):
                    last = mm(unit_ps[c % 3][:, hh * T:(hh + 1) * T], pick[:, 2 * c + hh, :], ndT[par][:],
                              start=True, stop=True)
                last.then_inc(s_db, 1)

            def transpose_probs(b, step, u, probs):
                if n_t.some_before(b, step, u, 1):
                    pe.wait_ge(s_pT, n_t.before(b, step, u, 1))
                for hh in range(2):
                    for kt in range(NT):
                        last = nc.tensor.transpose(pt_ps[u % 2][:, (2 * hh + kt) * P:(2 * hh + kt + 1) * P],
                                                   probs[:, u % 3, hh, kt * P:(kt + 1) * P], ident[:])
                last.then_inc(s_t, 1)

            def pt0(b, par, u):
                pe.wait_ge(s_p0, n_np0.after(b, "NORMP0", u))
                transpose_probs(b, "PT0", u, p0)

            def pt1(b, par, u):
                pe.wait_ge(s_e1, n_e1.after(b, "EXP1", u))
                transpose_probs(b, "PT1", u, p1)

            def pv0(b, par, p):
                pe.wait_ge(s_pT, n_t.after(b, "PT0", 2 * p + 1))
                bank, made = bank_free(b, "PV0", p, (("V", 0), ("V", 1)) if p == 0 else ())
                for kt in range(NT):
                    for hh in range(2):
                        h = 2 * p + hh
                        last = mm(bank[D0 * hh:D0 * (hh + 1), 0:T], vv[par][:, kt, h * D0:(h + 1) * D0],
                                  pT0[:, p % 2, hh, kt, :], start=kt == 0, stop=kt == NT - 1)
                last.then_inc(made, 1)

            def out0(b, par, t):
                first_use(b, t, WF)
                bank, made = bank_free(b, "OUT0", t, [("PV0", p) for p in range(3)] if t == 0 else ())
                to_rows(bank, c16, t, WF).then_inc(made, 1)

            def ln_t1(b, par, k):
                if k == 0:
                    pe.wait_ge(s_norm1, n_norm1.after(b, "NORM1"))
                bank, made = bank_free(b, "LN_T1", k)
                transpose_norm(bank, xn[1], k).then_inc(made, 1)

            def heads(b, par, t):
                first_use(b, t, WH)
                bank, made = bank_free(b, "HEADS", t, (("LN_T1", 0), ("LN_T1", 1)) if t == 0 else ())
                to_rows(bank, h16[1], t, WH).then_inc(made, 1)

            def gate_proj(b, par, t):
                first_use(b, t, WG)
                if b.ref == 0 and t == 0:
                    pe.wait_ge(s_gate_b, 1)
                bank, made = bank_free(b, "GATE", t)
                to_rows(bank, h16[1], t, WG, bias=True).then_inc(made, 1)

            def dst_t(b, par, _):
                bank, made, taken, _ = job(b, "DST_T")
                parts, free = ready(pe, n_sd.after(b, "SCORE_SUM")), ready(pe, n_job.before(b, "DST_T"))
                pe.wait_ge(s_pool_const, 8)
                pe.wait_ge(s_sd, parts)
                pe.wait_ge(taken, free)
                view = bank[:].bitcast(BF16)
                for t in range(NT):
                    last = nc.tensor.transpose(view[0:3 * H1, t * P:(t + 1) * P],
                                               nd_parts[:, t].rearrange("p a h -> p (a h)"), ident_b[:])
                last.then_inc(made, 1)

            def pv1(b, par, g):
                pe.wait_ge(s_pT, n_t.after(b, "PT1", 4 * g + 3))
                bank, made = bank_free(b, "PV1", g)
                for kt in range(NT):
                    for q in range(4):
                        h = 4 * g + q
                        last = mm(bank[D1 * q:D1 * (q + 1), 0:T], hv[par][:, kt, h * D1:(h + 1) * D1],
                                  pT1[:, g % 2, q, kt, :], start=kt == 0, stop=kt == NT - 1,
                                  tile_position=(0, D1 * q))
                last.then_inc(made, 1)

            def out_t(b, par, t):
                bank, made = bank_free(b, "OUT_T", t, [("PV1", g) for g in range(3)] if t == 0 else ())
                for g in range(3):
                    last = nc.tensor.transpose(bank[:, g * P:(g + 1) * P], oT[:, g, t * P:(t + 1) * P], ident[:])
                last.then_inc(made, 1)

            walk(pe, ORDERS["PE"],
                 {"LN_T0": ln_t0, "Q": to_columns("Q", WQ), "K": to_columns("K", WK), "V": v, "SCORES0": qk0,
                  "PT0": pt0, "PV0": pv0, "OUT0": out0, "LN_T1": ln_t1, "HEADS": heads, "GATE": gate_proj,
                  "DST_T": dst_t, "DST": dst, "PT1": pt1, "PV1": pv1, "OUT_T": out_t},
                 {-1: lambda: pe.wait_ge(s_rowdone, 1)})

        @block.scalar
        def _(act):
            op = nc.scalar.activation

            def sum_weight(w):
                if w:
                    act.wait_ge(s_wsum, w)
                act.wait_ge(s_w[w], 16)
                op(wabs, stage[w], ACT.Abs, accum_out=wsum[:, w:w + 1]).then_inc(s_wsum, 1)

            def high_weight(w):
                act.wait_ge(s_setup, SCALES_DONE[w // 2])
                op(w16[:, w, 0], stage[w], ACT.Copy, scale=wscale[:, w:w + 1]).then_inc(s_high, 1)

            for w in (WQ, WK):
                sum_weight(w)
            for w in (WF, WV):
                sum_weight(w)
            for w in (WQ, WK, WF, WV):
                high_weight(w)
            for w in (WH, WG):
                sum_weight(w)

            def made(b, step, idx=0):
                bank, full, taken, value = job(b, step, idx)
                act.wait_ge(full, value)
                return bank, taken

            def high_part(bank, h, k):
                c = slice(0, 2) if k == 0 else slice(2, 3)
                n = (c.stop - c.start) * T
                return op(h[:, 0, c, :], bank[:, 0:n].rearrange("p (c t) -> p c t", t=T), ACT.Relu)

            def ln_t0(b, par, k):
                high_part(made(b, "LN_T0", k)[0], h16[0], k).then_inc(s_hi0, 1)

            def ln_t1(b, par, k):
                high_part(made(b, "LN_T1", k)[0], h16[1], k).then_inc(s_hi1, 1)

            def q(b, par, p):
                if b.ref == 0 and p == 1:
                    high_weight(WH)
                    high_weight(WG)
                bank, taken = made(b, "Q", p)
                op(qT[par][:, p, :], bank[:, 0:T], ACT.Identity, bias=bq_c[:, p:p + 1],
                   scale=post_q[:]).then_inc(taken, 1)

            def v(b, par, t):
                bank, taken = made(b, "V", t)
                op(vv[par][:, t, :], bank[:, 0:H], ACT.Copy, scale=VS).then_inc(taken, 1)

            def exp0(b, par, u):
                act.wait_ge(s_y0, n_s0.after(b, "SCORES0", u))
                if n_t.some_before(b, "PT0", u, 2):
                    act.wait_ge(s_t, n_t.before(b, "PT0", u, 2))
                for hh in range(2):
                    last = op(p0[:, u % 3, hh, :], y0[:, u % YB, hh, :], ACT.Exp, bias=min0[:, u, hh:hh + 1],
                              scale=-1.0, accum_out=sum0[:, u, hh:hh + 1])
                last.then_inc(s_e0, 1)

            def pt0(b, par, u):
                p, qt = divmod(u, 2)
                act.wait_ge(s_t, n_t.after(b, "PT0", u))
                op(pT0[:, p % 2, :, :, qt * P:(qt + 1) * P],
                   pt_ps[u % 2][:].rearrange("p (h k q) -> p h k q", h=2, k=NT), ACT.Copy).then_inc(s_pT, 1)

            def pv0(b, par, p):
                bank, _ = made(b, "PV0", p)
                op(c16[:, 0, p, :], bank[:, 0:T], ACT.Copy).then_inc(s_hi0, 1)

            def heads(b, par, t):
                bank, taken = made(b, "HEADS", t)
                if t == 0 and b.ref >= 1:
                    act.wait_ge(s_prod, n_prod.after(b.back(1), "SCORE_PROD"))
                op(th[:, t, :], bank[:, 0:H], ACT.Tanh, scale=post[:, WH:WH + 1]).then_inc(s_th, 1)
                op(hv[par][:, t, :], bank[:, 0:H], ACT.Copy, scale=post[:, WH:WH + 1]).then_inc(taken, 1)

            def gate_(b, par, t):
                bank, taken = made(b, "GATE", t)
                if t == 0 and b.ref >= 1:
                    act.wait_ge(s_gate, n_gate.after(b.back(1), "GATES"))
                op(gtanh[:, t, :], bank[:, 0:H], ACT.Tanh, scale=post_g[:]).then_inc(taken, 1)

            def dst(b, par, c):
                act.wait_ge(s_db, n_db.after(b, "DST", c))
                if n_y1.some_before(b, "SCORES1", 2 * c, 2):
                    act.wait_ge(s_y1, n_y1.before(b, "SCORES1", 2 * c, 2))
                op(dst5[:, c % 2].rearrange("p h t -> p (h t)"), unit_ps[c % 3][:], ACT.Copy,
                   scale=ALPHA).then_inc(s_d5, 1)

            def exp1(b, par, u):
                c, t = divmod(u, 2)
                act.wait_ge(s_y1, n_y1.after(b, "SCORES1", u))
                if n_t.some_before(b, "PT1", u, 2):
                    act.wait_ge(s_t, n_t.before(b, "PT1", u, 2))
                if u == 0 and b.ref >= 1:
                    act.wait_ge(s_rec1, n_rec1.after(b.back(1), "RECIP1"))
                for hh in range(2):
                    h = 2 * c + hh
                    last = op(p1[:, u % 3, hh, :], y1[:, u % YB, hh, :], ACT.Exp, bias=min1[:, u, hh:hh + 1],
                              scale=-1.0, accum_out=sum1[:, t, h:h + 1])
                last.then_inc(s_e1, 1)

            def pt1(b, par, u):
                c, t = divmod(u, 2)
                g, q_ = divmod(2 * c, 4)
                act.wait_ge(s_t, n_t.after(b, "PT1", u))
                op(pT1[:, g % 2, q_:q_ + 2, :, t * P:(t + 1) * P],
                   pt_ps[u % 2][:].rearrange("p (h k q) -> p h k q", h=2, k=NT), ACT.Copy).then_inc(s_pT, 1)

            def elu_relu(b, par, _):
                act.wait_ge(s_ob, n_ob.after(b, "ELU_BIAS"))
                op(o1m[:], o1[:], ACT.Relu, scale=-1.0).then_inc(s_om, 1)

            def elu_exp(b, par, _):
                act.wait_ge(s_om, n_om.after(b, "ELU_RELU"))
                op(o1m[:], o1m[:], ACT.Exp, scale=-1.0).then_inc(s_oe, 1)

            walk(act, ORDERS["ACT"], {"LN_T0": ln_t0, "Q": q, "V": v, "EXP0": exp0, "PT0": pt0, "PV0": pv0, "LN_T1": ln_t1,
                       "HEADS": heads, "GATE": gate_, "DST": dst, "EXP1": exp1, "PT1": pt1,
                       "ELU_RELU": elu_relu, "ELU_EXP": elu_exp})

        @block.vector
        def _(dve):
            chain = [0]

            def own(ins):
                chain[0] += 1
                ins.then_inc(s_setup, 1)
                dve.wait_ge(s_setup, chain[0])

            V = nc.vector
            dve.wait_ge(s_small, 16 * 8)
            for c in range(NC):
                last = V.tensor_copy(bv_w[:, c, :], bv_c[:, c:c + 1].broadcast_to([P, P]))
            last.then_inc(s_bvw, 1)
            own(V.tensor_scalar(bq_c[:], bq_c[:], -1.0 / 8.0, None, ALU.mult))
            own(V.tensor_scalar(src_row[:], src_row[:], -(1.0 - ALPHA), None, ALU.mult))
            own(V.tensor_scalar(dst_row[:], dst_row[:], -1.0, None, ALU.mult))

            def scales(pair):
                at = slice(2 * pair, 2 * pair + 2)
                dve.wait_ge(s_wsum_all, pair + 1)
                own(V.tensor_scalar(wsum_all[:, at], wsum_all[:, at], 1e-30, None, ALU.max))
                own(V.reciprocal(wscale[:, at], wsum_all[:, at]))
                own(V.tensor_scalar(wscale[:, at], wscale[:, at], WS, None, ALU.mult))
                own(V.reciprocal(post[:, at], wscale[:, at]))
                own(V.tensor_scalar(post[:, at], post[:, at], 1.0 / XS, None, ALU.mult))
                if pair == WQ // 2:
                    own(V.tensor_scalar(post_q[:], post[:, WQ:WQ + 1], -1.0 / 8.0, None, ALU.mult))
                if pair == WF // 2:
                    own(V.tensor_tensor(post_f[:], post[:, WV:WV + 1], post[:, WF:WF + 1], ALU.mult))
                    own(V.tensor_scalar(post_f[:], post_f[:], XS / VS, None, ALU.mult))
                assert chain[0] == SCALES_DONE[pair]

            def low_weight(w):
                dve.wait_ge(s_high, w + 1)
                V.scalar_tensor_tensor(w16[:, w, 1], stage[w], wscale[:, w:w + 1], w16[:, w, 0],
                                       ALU.mult, ALU.subtract).then_inc(s_w16, 1)

            def first_weights():
                low_weight(WQ)
                low_weight(WK)

            def next_weights():
                low_weight(WF)
                low_weight(WV)
                dve.wait_ge(s_row, 1)
                V.tensor_tensor(out0_row[:], pt_ps[0][:, 0:H], out0_row[:], ALU.add).then_inc(s_rowdone, 1)

            def gate_bias():
                own(V.tensor_scalar(gate_b_row[:], gate_b_row[:], wscale[:, WG:WG + 1], XS, ALU.mult, ALU.mult))
                for k in range(3):
                    own(V.tensor_copy(gate_part[:], gate_b_row[:]))
                    if k == 0:
                        own(V.tensor_scalar(gate_b3[:], gate_part[:], ident[:, 0:1], None, ALU.mult))
                    else:
                        own(V.scalar_tensor_tensor(gate_b3[:], gate_part[:], ident[:, k:k + 1], gate_b3[:],
                                                   ALU.mult, ALU.add))
                    if k < 2:
                        own(V.tensor_tensor(gate_b_row[:], gate_b_row[:], gate_part[:], ALU.subtract))
                V.tensor_scalar(post_g[:], post[:, WG:WG + 1], 0.5, None, ALU.mult).then_inc(s_gate_b, 1)

            scales(0)
            scales(1)

            def aggregate(b, k, step, idx=0):
                written = ready(dve, n_bn.after(b, step, idx))
                dve.wait_ge(s_pool_const, 8)
                dve.wait_ge(s_bn, written)
                for t in range(NT):
                    last = V.bn_aggr(mv[k][:, t, :], bn[k][:, t, :])
                last.then_inc(s_mv, 1)

            def stats0(b, par, _):
                dve.wait_ge(s_x[par], loaded(b))
                for t in range(NT):
                    last = V.bn_stats(bn[0][:, t, :], xb[par][:, t, :])
                last.then_inc(s_bn, 1)
                aggregate(b, 0, "STATS0")
                if b.ref == 0:
                    first_weights()

            def stats1(b, par, t):
                _, _, taken, value = job(b, "OUT0", t)
                dve.wait_ge(taken, value)
                V.bn_stats(bn[1][:, t, :], x2[par][:, t, :]).then_inc(s_bn, 1)

            def aggregate1(b, par, _):
                aggregate(b, 1, "STATS1", 1)

            def norm1(b, par, _):
                dve.wait_ge(s_rstd, n_rstd.after(b, "RSTD1"))
                for t in range(NT):
                    last = V.tensor_scalar(xn[1][:, t, :], x2[par][:, t, :], mv[1][:, t, 0:1], rstd[1][:, t:t + 1],
                                           ALU.subtract, ALU.mult)
                last.then_inc(s_norm1, 1)

            def made(b, step, idx=0):
                bank, full, taken, value = job(b, step, idx)
                dve.wait_ge(full, value)
                return bank, taken

            def low_part(b, step, h, k):
                bank, _, taken, _ = job(b, step, k)
                c = slice(0, 2) if k == 0 else slice(2, 3)
                n = (c.stop - c.start) * T
                V.scalar_tensor_tensor(h[:, 1, c, :].rearrange("p c t -> p (c t)"), bank[:, 0:n], 0.0,
                                       h[:, 0, c, :].rearrange("p c t -> p (c t)"),
                                       ALU.max, ALU.subtract).then_inc(taken, 1)

            def ln_t0(b, par, k):
                dve.wait_ge(s_hi0, n_hi0.after(b, "LN_T0", k))
                low_part(b, "LN_T0", h16[0], k)
                if b.ref == 0 and k == 1:
                    next_weights()

            def ln_t1(b, par, k):
                dve.wait_ge(s_hi1, n_hi1.after(b, "LN_T1", k))
                low_part(b, "LN_T1", h16[1], k)

            def k_(b, par, p):
                bank, taken = made(b, "K", p)
                for hh in range(2):
                    r = slice(D0 * hh, D0 * (hh + 1))
                    last = V.tensor_scalar(kz[par][r, 2 * p + hh, :], bank[r, 0:T], post[r, WK:WK + 1],
                                           bk_c[r, p:p + 1], ALU.mult, ALU.add)
                last.then_inc(taken, 1)
                if b.ref == 0 and p == 0:
                    scales(WH // 2)
                if b.ref == 0 and p == 1:
                    low_weight(WH)
                    low_weight(WG)
                    gate_bias()

            def qk0(b, par, u):
                qt = u % 2
                masks = ready(dve, n_mask0.after(b, "MASK0"))
                scores = ready(dve, n_s0.after(b, "SCORES0", u))
                used = ready(dve, n_e0.before(b, "EXP0", u, YB - 1))
                dve.wait_ge(s_pool_const, 8)
                if u == 0:
                    dve.wait_ge(s_mask0, masks)
                dve.wait_ge(s_s0, scores)
                if n_e0.some_before(b, "EXP0", u, YB - 1):
                    dve.wait_ge(s_e0, used)
                for hh in range(2):
                    last = V.tensor_tensor_reduce(y0[:, u % YB, hh, :], unit_ps[u % 3][:, hh * T:(hh + 1) * T],
                                                  mask0[:, qt, :], 1.0, 3.0e38, ALU.add, ALU.min,
                                                  min0[:, u, hh:hh + 1])
                last.then_inc(s_y0, 1)

            def normp0(b, par, u):
                dve.wait_ge(s_e0, n_e0.after(b, "EXP0", u))
                V.reciprocal(rec0[:, u, :], sum0[:, u, :]).then_inc(s_rec0, 1)

            def pv0(b, par, p):
                dve.wait_ge(s_hi0, n_hi0.after(b, "PV0", p))
                bank, _, taken, _ = job(b, "PV0", p)
                V.tensor_tensor(c16[:, 1, p, :], bank[:, 0:T], c16[:, 0, p, :], ALU.subtract).then_inc(taken, 1)

            def out0(b, par, t):
                bank, taken = made(b, "OUT0", t)
                if t == 0:
                    dve.wait_ge(s_xc, n_xc.after(b, "RES_ROW"))
                    if b.ref >= 2:
                        dve.wait_ge(s_skip, n_skip.after(b.back(2), "SKIP"))
                V.scalar_tensor_tensor(x2[par][:, t, :], bank[:, 0:H], post_f[:], xc[:, t, :],
                                       ALU.mult, ALU.add).then_inc(taken, 1)

            def skip_h(b, par, _):
                dve.wait_ge(s_norm1, n_norm1.after(b, "NORM1"))
                if b.ref >= 1:
                    dve.wait_ge(s_ungate, n_ungate.after(b.back(1), "SKIP"))
                V.tensor_scalar(hskip[:], xn[1][:], 0.0, 1.0 / XS, ALU.max, ALU.mult).then_inc(s_hskip, 1)

            def score_sum(b, par, _):
                dve.wait_ge(s_halves, n_halves.after(b, "SCORE_PROD"))
                for i, dst_ in enumerate((s8[par], nd)):
                    V.reduce_sum(dst_[:].rearrange("p t h -> p (t h)"),
                                 prod[:, i].rearrange("p t (h e) -> p (t h) e", e=D1)[:, :, 0:D1 // 2],
                                 AX_X).then_inc(s_sd, 1)
                dve.wait_ge(s_sd, n_sd.after(b, "SCORE_SUM", 0, 2))
                V.tensor_copy(nd_parts[:, :, 0, :], nd[:]).then_inc(s_sd, 1)
                dve.wait_ge(s_sd, n_sd.after(b, "SCORE_SUM", 0, 3))
                V.tensor_tensor(nd_r[:], nd[:], nd_parts[:, :, 0, :], ALU.subtract).then_inc(s_sd, 1)
                dve.wait_ge(s_sd, n_sd.after(b, "SCORE_SUM", 0, 4))
                V.tensor_copy(nd_parts[:, :, 1, :], nd_r[:]).then_inc(s_nd, 1)
                dve.wait_ge(s_nd, n_nd.after(b, "SCORE_SUM"))
                V.tensor_tensor(nd_parts[:, :, 2, :], nd_r[:], nd_parts[:, :, 1, :], ALU.subtract).then_inc(s_sd, 1)

            def dst_t(b, par, _):
                bank, taken = made(b, "DST_T")
                V.tensor_copy(ndT[par][0:3 * H1, :], bank[:].bitcast(BF16)[0:3 * H1, 0:T]).then_inc(taken, 1)

            def leaky1(b, par, u):
                c, t = divmod(u, 2)
                if u == 0:
                    dve.wait_ge(s_mask1, n_mask1.after(b, "MASK1"))
                if t == 0:
                    dve.wait_ge(s_d5, n_db.after(b, "DST", c))
                if n_e1.some_before(b, "EXP1", u, YB - 1):
                    dve.wait_ge(s_e1, n_e1.before(b, "EXP1", u, YB - 1))
                for hh in range(2):
                    h = 2 * c + hh
                    V.scalar_tensor_tensor(yw[:, u % 2, hh, :], unit_ps[c % 3][:, hh * T:(hh + 1) * T],
                                           s8[par][:, t, h:h + 1], dst5[:, c % 2, hh, :],
                                           ALU.add, ALU.min).then_inc(s_lk, 1)
                for hh in range(2):
                    written = ready(dve, n_lk.after(b, "SCORES1", u, hh + 1))
                    dve.wait_ge(s_pool_const, 8)
                    dve.wait_ge(s_lk, written)
                    last = V.tensor_tensor_reduce(y1[:, u % YB, hh, :], yw[:, u % 2, hh, :], mask1[:, t, :],
                                                  1.0, 3.0e38, ALU.add, ALU.min, min1[:, u, hh:hh + 1])
                last.then_inc(s_y1, 1)

            def pv1(b, par, g):
                bank, taken = made(b, "PV1", g)
                V.tensor_copy(oT[:, g, :], bank[:, 0:T]).then_inc(taken, 1)

            def recip1(b, par, _):
                dve.wait_ge(s_e1, n_e1.after(b, "EXP1", 11))
                V.reciprocal(rec1[:].rearrange("p t h -> p (t h)"),
                             sum1[:].rearrange("p t h -> p (t h)")).then_inc(s_rec1, 1)

            def out_t(b, par, t):
                bank, taken = made(b, "OUT_T", t)
                if t == 0:
                    dve.wait_ge(s_rec1, n_rec1.after(b, "RECIP1"))
                V.tensor_tensor(o1[:, t, :].rearrange("p (h e) -> p h e", e=D1),
                                bank[:, 0:H].rearrange("p (h e) -> p h e", e=D1),
                                rec1[:, t, :].unsqueeze(2).broadcast_to([P, H1, D1]), ALU.mult).then_inc(taken, 1)

            def finish(b, par, k):
                if k == 0:
                    dve.wait_ge(s_oe, n_oe.after(b, "ELU_EXP"))
                    V.scalar_tensor_tensor(o1m[:], o1[:], 0.0, o1m[:], ALU.max, ALU.add).then_inc(s_fin, 1)
                else:
                    dve.wait_ge(s_fin, n_fin.after(b, "FINISH", 0))
                    if b.ref >= 1:
                        dve.wait_ge(s_out, n_out.after(b.back(1), "STORE"))
                    V.scalar_tensor_tensor(y[:], o1m[:], -1.0, gate[par][:], ALU.add, ALU.mult).then_inc(s_fin, 1)

            walk(dve, ORDERS["DVE"], {"STATS0": stats0, "LN_T0": ln_t0,
                       "K": k_, "SCORES0": qk0, "NORMP0": normp0, "PV0": pv0, "OUT0": out0,
                       "STATS1": stats1, "AGGREGATE1": aggregate1, "NORM1": norm1, "LN_T1": ln_t1,
                       "SCORE_SUM": score_sum, "DST_T": dst_t, "SCORES1": leaky1,
                       "PV1": pv1, "RECIP1": recip1, "OUT_T": out_t, "FINISH": finish, "SKIP_H": skip_h})

        @block.gpsimd
        def _(pool):
            G = nc.gpsimd
            G.memset(ident[:], 0.0).then_inc(s_pool_const, 1)
            G.memset(pick[:], 0.0).then_inc(s_pool_const, 1)
            G.memset(ones_b[:], 1.0)
            G.memset(half[:], -0.5).then_inc(s_pool_const, 1)
            pool.wait_ge(s_pool_const, 3)
            G.affine_select(out=ident[:], in_=ident[:], compare_op=ALU.not_equal, fill=1.0, base=0,
                            pattern=[[-1, P]], channel_multiplier=1).then_inc(s_pool_const, 1)
            for i in range(3):
                G.affine_select(out=pick[:], in_=pick[:], compare_op=ALU.not_equal, fill=1.0, base=-H1 * i,
                                pattern=[[-1, H1], [0, P]], channel_multiplier=1).then_inc(s_pool_const, 1)
                pool.wait_ge(s_pool_const, 5 + i)

            def largest_sums(pair):
                at = slice(2 * pair, 2 * pair + 2)
                pool.wait_ge(s_wsum, 2 * pair + 2)
                G.partition_all_reduce(wsum_all[:, at], wsum[:, at], P, RMAX).then_inc(s_wsum_all, 1)

            largest_sums(0)
            for i in range(2):
                G.memset(kz[i][:], 0.0)
                G.memset(ndT[i][:], 0.0)
            G.tensor_copy(ident_b[:], ident[:]).then_inc(s_pool_const, 1)
            largest_sums(1)

            def make_mask0(b, par, _):
                here = ready(pool, loaded(b))
                read = ready(pool, n_s0.after(b.back(1), "SCORES0", 5)) if b.ref >= 1 else None
                pool.wait_ge(s_pool_const, 8)
                pool.wait_ge(s_adj[par], here)
                if b.ref >= 1:
                    pool.wait_ge(s_y0, read)
                G.tensor_scalar(mask0[:], adj_raw[par][:], -1.0, -BIG, ALU.add, ALU.mult).then_inc(s_mask0, 1)

            def make_mask1(b, par, _):
                here = ready(pool, loaded(b))
                read = ready(pool, n_y1.after(b.back(1), "SCORES1", 11)) if b.ref >= 1 else None
                pool.wait_ge(s_pool_const, 8)
                pool.wait_ge(s_adj[par], here)
                if b.ref >= 1:
                    pool.wait_ge(s_y1, read)
                G.tensor_scalar(mask1[:], adj_raw[par][:], -1.0, -BIG, ALU.add, ALU.mult).then_inc(s_mask1, 1)

            def make_rstd(k, step, sstep):
                def part(b, par, _):
                    here = ready(pool, n_mv.after(b, sstep))
                    pool.wait_ge(s_pool_const, 8)
                    pool.wait_ge(s_mv, here)
                    if k == 0:
                        G.tensor_scalar(nmean[:], mv[0][:, :, 0], -1.0, 1.0, ALU.mult, ALU.mult)
                    G.tensor_scalar(veps[:, k, :], mv[k][:, :, 1], EPS, XS ** -2, ALU.add, ALU.mult).then_inc(s_veps, 1)
                    pool.wait_ge(s_veps, n_veps.after(b, step))
                    G.tensor_tensor(rstd[k][:], veps[:, k, :], half[:], ALU.pow).then_inc(s_rstd, 1)
                return part

            def norm0(b, par, _):
                here = ready(pool, n_rstd.after(b, "RSTD0"))
                if b.ref >= 1:
                    _, made, _, value = job(b.back(1), "LN_T0", 1)
                    used = ready(pool, value)
                pool.wait_ge(s_pool_const, 8)
                pool.wait_ge(s_rstd, here)
                if b.ref >= 1:
                    pool.wait_ge(made, used)
                for t in range(NT):
                    last = G.tensor_scalar(xn[0][:, t, :], xb[par][:, t, :], nmean[:, t:t + 1], rstd[0][:, t:t + 1],
                                           ALU.add, ALU.mult)
                last.then_inc(s_norm0, 1)

            def normp0(b, par, u):
                here = ready(pool, n_np0.after(b, "NORMP0", u))
                pool.wait_ge(s_pool_const, 8)
                pool.wait_ge(s_rec0, here)
                for hh in range(2):
                    last = G.tensor_scalar(p0[:, u % 3, hh, :], p0[:, u % 3, hh, :], rec0[:, u, hh:hh + 1], 1.0,
                                           ALU.mult, ALU.mult)
                last.then_inc(s_p0, 1)

            def res_row(b, par, _):
                pool.wait_ge(s_x[par], loaded(b))
                if b.ref == 0:
                    pool.wait_ge(s_rowdone, 1)
                else:
                    for t in range(NT):
                        _, _, taken, value = job(b.back(1), "OUT0", t)
                        pool.wait_ge(taken, value)
                G.tensor_tensor(xc[:], xb[par][:], out0_row[:].unsqueeze(1).broadcast_to([P, NT, H]),
                                ALU.add).then_inc(s_xc, 1)

            def score_prod(b, par, _):
                pool.wait_ge(s_th, n_th.after(b, "HEADS", 1))
                if b.ref >= 1:
                    pool.wait_ge(s_sd, n_sd.after(b.back(1), "SCORE_SUM"))
                else:
                    pool.wait_ge(s_setup, 3)
                for i, row in enumerate((src_row, dst_row)):
                    last = G.tensor_tensor(prod[:, i], th[:], row[:].unsqueeze(1).broadcast_to([P, NT, H]), ALU.mult)
                last.then_inc(s_prod, 1)
                pool.wait_ge(s_prod, n_prod.after(b, "SCORE_PROD"))
                halves = [prod[:].rearrange("p i t (h e) -> p (i t h) e", e=D1)[:, :, k * D1 // 2:(k + 1) * D1 // 2]
                          for k in range(2)]
                G.tensor_tensor(halves[0], halves[0], halves[1], ALU.add).then_inc(s_halves, 1)

            def gates(b, par, _):
                jobs_ = [job(b, "GATE", t) for t in range(NT)]
                tanh = [ready(pool, value) for _, _, _, value in jobs_]
                used = ready(pool, n_fin.after(b.back(2), "FINISH", 1)) if b.ref >= 2 else None
                pool.wait_ge(s_pool_const, 8)
                for (_, _, taken, _), value in zip(jobs_, tanh):
                    pool.wait_ge(taken, value)
                if b.ref >= 2:
                    pool.wait_ge(s_fin, used)
                G.tensor_scalar(gate[par][:], gtanh[:], 0.5, 0.5, ALU.mult, ALU.add)
                G.tensor_scalar(ungate[:], gtanh[:], -0.5, 0.5, ALU.mult, ALU.add).then_inc(s_gate, 1)

            def skip(b, par, _):
                pool.wait_ge(s_gate, n_gate.after(b, "GATES"))
                pool.wait_ge(s_hskip, n_hskip.after(b, "SKIP_H"))
                G.tensor_tensor(ungate[:], ungate[:], hskip[:], ALU.mult).then_inc(s_ungate, 1)
                pool.wait_ge(s_ungate, n_ungate.after(b, "SKIP"))
                G.tensor_tensor(xskip[par][:], ungate[:], x2[par][:], ALU.add).then_inc(s_skip, 1)

            def elu_bias(b, par, _):
                for t in range(NT):
                    _, _, taken, value = job(b, "OUT_T", t)
                    pool.wait_ge(taken, value)
                G.tensor_tensor(o1[:].rearrange("p t (h e) -> p (t h) e", e=D1),
                                o1[:].rearrange("p t (h e) -> p (t h) e", e=D1),
                                gat_b_row[:].unsqueeze(1).broadcast_to([P, NT * H1, D1]), ALU.add).then_inc(s_ob, 1)

            def out_sum(b, par, _):
                pool.wait_ge(s_fin, n_fin.after(b, "FINISH", 1))
                G.tensor_tensor(y[:], y[:], xskip[par][:], ALU.add).then_inc(s_sum, 1)

            walk(pool, ORDERS["POOL"],
                 {"MASK0": make_mask0, "MASK1": make_mask1, "RSTD0": make_rstd(0, "RSTD0", "STATS0"),
                  "RSTD1": make_rstd(1, "RSTD1", "AGGREGATE1"), "NORM0": norm0, "NORMP0": normp0, "RES_ROW": res_row,
                  "SCORE_PROD": score_prod, "GATES": gates, "SKIP": skip, "ELU_BIAS": elu_bias,
                  "OUT_SUM": out_sum},
                 {-1: lambda: largest_sums(2)})


SCALES_DONE = (3 + 6, 3 + 6 + 7, 3 + 6 + 7 + 5)

_INS = ["x", "adj", "w_all", "bq", "bk", "bv", "bf", "gat_b", "w_src", "w_dst", "gate_b"]


def kernel(x, adj, L0_gnn_Wq, L0_gnn_bq, L0_gnn_Wk, L0_gnn_bk, L0_gnn_Wv, L0_gnn_bv, L0_gnn_Wf, L0_gnn_bf,
           L1_gnn_W, L1_gnn_b, L1_gnn_w_src, L1_gnn_w_dst, L1_gnn_H_w, L1_gnn_H_b):
    import concourse.bacc as bacc
    from concourse.bass_utils import run_bass_kernel_spmd

    heads_w = np.asarray(L1_gnn_W).transpose(1, 0, 2).reshape(H, H)


    def columns(a):
        return np.asarray(a).reshape(NC, P).T

    given = {
        "x": x, "adj": adj,
        "w_all": np.stack([np.asarray(L0_gnn_Wq), np.asarray(L0_gnn_Wk), np.asarray(L0_gnn_Wf),
                           np.asarray(L0_gnn_Wv), heads_w, np.asarray(L1_gnn_H_w).T]),
        "bq": columns(L0_gnn_bq), "bk": columns(L0_gnn_bk), "bv": columns(L0_gnn_bv), "bf": L0_gnn_bf, "gat_b": L1_gnn_b,
        "w_src": np.asarray(L1_gnn_w_src).reshape(H), "w_dst": np.asarray(L1_gnn_w_dst).reshape(H),
        "gate_b": L1_gnn_H_b,
    }
    nc = bacc.Bacc("TRN2", target_bir_lowering=False, num_devices=1)
    arrays, args = {}, []
    for name in _INS:
        a = np.ascontiguousarray(given[name])
        arrays[f"in_{name}_dram"] = a
        args.append(nc.dram_tensor(f"in_{name}_dram", a.shape, mybir.dt.from_np(a.dtype), kind="ExternalInput").ap())
    out = nc.dram_tensor("out_dram", np.asarray(x).shape, F32, kind="ExternalOutput").ap()
    build(nc, *args, out)
    r = run_bass_kernel_spmd(nc, [arrays], core_ids=[0])
    return r.results[0]["out_dram"]
```
